# Optimizing a Trainium2 kernel written in Bass

```python
import numpy as np
import jax
import jax.numpy as jnp

def _softmax(x, axis=-1):
    return jax.nn.softmax(x, axis=axis)

def _gelu(x):
    return jax.nn.gelu(x, approximate=True)

def _silu(x):
    return jax.nn.silu(x)

def _sigmoid(x):
    return jax.nn.sigmoid(x)

def _layernorm(x, axis=-1, eps=1e-05):
    m = jnp.mean(x, axis=axis, keepdims=True)
    v = jnp.var(x, axis=axis, keepdims=True)
    return (x - m) / jnp.sqrt(v + eps)

def _scatter_add(tgt, idx, src, axis=0):
    return tgt.at[idx].add(src)

def _segment_sum(src, seg, n):
    return jax.ops.segment_sum(src, seg, n)
kernel_name = 'mk_gnn_preln_d1_gnn_r32_28278c'

def setup_inputs(seed: int=0):
    np.random.seed(seed)
    _w = jnp.asarray

    def _rec_inputs():
        import jax
        import jax.numpy as jnp
        _gk = jax.random.key(seed)
        x = -0.0003929 + 0.9999 * jax.random.normal(jax.random.fold_in(_gk, 1), (1024, 512), jnp.float32)
        _s = jax.random.randint(jax.random.fold_in(_gk, 2), (16384,), 0, 1024, jnp.int32)
        _d = jax.random.randint(jax.random.fold_in(_gk, 3), (16384,), 0, 1024, jnp.int32)
        _loop = jnp.arange(1024, dtype=jnp.int32)
        src = jnp.concatenate([_s, _d, _loop])
        dst = jnp.concatenate([_d, _s, _loop])
        _o = jnp.argsort(dst, stable=True)
        src = src[_o]
        dst = dst[_o]
        edge_weight = jax.random.uniform(jax.random.fold_in(_gk, 13), (33792,), jnp.float32, 0.0, 0.999999)
        return (x, src, dst, edge_weight)
    x, src, dst, edge_weight = _rec_inputs()

    def _L0_gnn_setup():
        import jax, jax.numpy as jnp
        import numpy as np
        N = 1024
        E = 16384
        D = 512
        G = 512
        key = jax.random.key(seed)
        ks = jax.random.split(key, 16)
        inp = {'feat': jax.random.normal(ks[0], (N, D), jnp.float32), 'src': jax.random.randint(ks[1], (E,), 0, N, jnp.int32), 'dst': jax.random.randint(ks[2], (E,), 0, N, jnp.int32), 'adj_vals': jax.random.uniform(ks[3], (E,), jnp.float32), 'graph_ids': jnp.arange(N, dtype=jnp.int32) // (N // G), 'W0': jax.random.normal(ks[4], (D, D), jnp.float32) * 0.05, 'b0': jnp.zeros((D,), jnp.float32), 'W1': jax.random.normal(ks[5], (D, D), jnp.float32) * 0.05, 'b1': jnp.zeros((D,), jnp.float32), 'gW1': jax.random.normal(ks[6], (D, D), jnp.float32) * 0.05, 'gb1': jnp.zeros((D,), jnp.float32), 'gW2': jax.random.normal(ks[7], (D, D), jnp.float32) * 0.05, 'gb2': jnp.zeros((D,), jnp.float32), 'gW3': jax.random.normal(ks[8], (D, D), jnp.float32) * 0.05, 'gb3': jnp.zeros((D,), jnp.float32), 'gWs': jax.random.normal(ks[9], (D, D), jnp.float32) * 0.05, 'gbs': jnp.zeros((D,), jnp.float32)}
        return inp
    _L0_gnn_all = _L0_gnn_setup()
    _L0_gnn_in = {k: v for k, v in _L0_gnn_all.items() if k in ('W0', 'b0', 'W1', 'b1', 'gW1', 'gb1', 'gW2', 'gb2', 'gW3', 'gb3', 'gWs', 'gbs')}
    del _L0_gnn_all
    return {'x': x, 'src': src, 'dst': dst, 'edge_weight': edge_weight, 'L0_gnn_W0': _L0_gnn_in['W0'], 'L0_gnn_b0': _L0_gnn_in['b0'], 'L0_gnn_W1': _L0_gnn_in['W1'], 'L0_gnn_b1': _L0_gnn_in['b1'], 'L0_gnn_gW1': _L0_gnn_in['gW1'], 'L0_gnn_gb1': _L0_gnn_in['gb1'], 'L0_gnn_gW2': _L0_gnn_in['gW2'], 'L0_gnn_gb2': _L0_gnn_in['gb2'], 'L0_gnn_gW3': _L0_gnn_in['gW3'], 'L0_gnn_gb3': _L0_gnn_in['gb3'], 'L0_gnn_gWs': _L0_gnn_in['gWs'], 'L0_gnn_gbs': _L0_gnn_in['gbs']}

def reference(x, src, dst, edge_weight, L0_gnn_W0, L0_gnn_b0, L0_gnn_W1, L0_gnn_b1, L0_gnn_gW1, L0_gnn_gb1, L0_gnn_gW2, L0_gnn_gb2, L0_gnn_gW3, L0_gnn_gb3, L0_gnn_gWs, L0_gnn_gbs):
    import jax
    import jax.numpy as jnp

    def _L0_gnn_ref(feat, src, dst, adj_vals, graph_ids, W0, b0, W1, b1, gW1, gb1, gW2, gb2, gW3, gb3, gWs, gbs):
        import jax, jax.numpy as jnp
        import numpy as np
        N = 1024
        E = 16384
        D = 512
        G = 512

        def gcn(h, W, b, act):
            support = h @ W
            msg = adj_vals[:, None] * support[src]
            agg = jax.ops.segment_sum(msg, dst, num_segments=N)
            return act(agg + b)
        h = gcn(feat, W0, b0, jax.nn.relu)
        h = gcn(h, W1, b1, lambda x: x)
        ones = jnp.ones((N, 1), h.dtype)
        counts = jax.ops.segment_sum(ones, graph_ids, num_segments=G)
        pooled = jax.ops.segment_sum(h, graph_ids, num_segments=G) / counts
        g = jax.nn.sigmoid(pooled)[graph_ids]
        z = jax.nn.relu(g @ gW1 + gb1)
        z = jax.nn.relu(z @ gW2 + gb2)
        z = jax.nn.relu(z @ gW3 + gb3)
        return z + (g @ gWs + gbs)
    batch0 = jnp.zeros((1024,), jnp.int32)
    h = jnp.maximum(_layernorm(x, axis=-1), 0.0)
    x = x + _L0_gnn_ref(h, src, dst, edge_weight, batch0, L0_gnn_W0, L0_gnn_b0, L0_gnn_W1, L0_gnn_b1, L0_gnn_gW1, L0_gnn_gb1, L0_gnn_gW2, L0_gnn_gb2, L0_gnn_gW3, L0_gnn_gb3, L0_gnn_gWs, L0_gnn_gbs)
    return x

_drawn_inputs = setup_inputs


def setup_inputs(seed=0):
    import zlib

    import numpy as np

    out = dict(_drawn_inputs(seed))
    spreads = {'L0_gnn_b0': (0.0, 0.288),
     'L0_gnn_b1': (0.0, 0.8),
     'L0_gnn_gb1': (0.0, 0.1),
     'L0_gnn_gb2': (0.0, 0.1),
     'L0_gnn_gb3': (0.0, 0.1),
     'L0_gnn_gbs': (0.0, 0.1)}
    factors = {'edge_weight': 5.952}
    for name, (base, spread) in spreads.items():
        noise = np.random.default_rng([zlib.crc32(name.encode()), seed]).standard_normal(out[name].shape)
        drawn = base * np.exp(spread * noise) if base else spread * noise
        out[name] = jnp.asarray(drawn.astype(out[name].dtype))
    for name, factor in factors.items():
        out[name] = (out[name] * factor).astype(out[name].dtype)
    return out
```

```python
import concourse.bass as bass
from concourse import mybir
from contextlib import ExitStack

F32 = mybir.dt.float32
BF16 = mybir.dt.bfloat16
I32 = mybir.dt.int32
U32 = mybir.dt.uint32
ALU = mybir.AluOpType
ACT = mybir.ActivationFunctionType
AX_X = mybir.AxisListType.X

P = 128


def gnn_block(nc, x, src, dst, edge_weight, W0, b0, W1, b1, gW1, gb1, gW2, gb2, gW3, gb3, gWs, gbs, out):
    N, D = x.shape
    E = src.shape[0]
    MT = N // P
    FT = D // P
    WIN = 8
    NW = N // WIN
    CH = 3
    CAP = CH * P
    KEYS = WIN * MT
    GW = P // WIN
    NG = NW // GW
    NH = 2 * NG
    HD = P // 2
    HC = GW // 2 * CH
    EP = E // P
    BLK = 24
    NB = EP // BLK
    EPS = 1e-5
    assert NW == P and KEYS * GW == 2 * 512 and EP % BLK == 0 and CAP % BLK == 0 and NG % 2 == 0

    ctx = ExitStack()
    with ctx:
        def sb(name, shape, dt=F32):
            return ctx.enter_context(nc.sbuf_tensor(name, shape, dt))

        def ps(name, shape, dt=F32):
            return ctx.enter_context(nc.psum_tensor(name, shape, dt))

        def sem(name):
            return ctx.enter_context(nc.semaphore(name))

        iota_bf = sb("iota_bf", [P, P], BF16)
        iota_8t = sb("iota_8t", [P, P], BF16)
        iota_key = sb("iota_key", [P, 512])
        win_base = sb("win_base", [P, 1])
        ident_bf = sb("ident_bf", [P, P], BF16)
        ident = sb("ident", [P, P])
        ones_bf = sb("ones_bf", [P, P], BF16)
        ones_row = sb("ones_row", [1, P])
        node_count = sb("node_count", [1, 1])
        blk_cols = sb("blk_cols", [P, NB, 3], BF16)
        dst_flat = sb("dst_flat", [P, EP], I32)
        src_flat = sb("src_flat", [P, EP], I32)
        w_flat = sb("w_flat", [P, EP])
        blk_min = sb("blk_min", [P, NB])
        blk_max = sb("blk_max", [P, NB])
        below = sb("below", [P, 2, NB, P], BF16)
        cnt = sb("cnt", [P, 2, 3])
        chk = sb("chk", [P, 16])
        in_order = sb("in_order", [P, 1], BF16)
        start = sb("start", [P, 1], U32)
        flag = sb("flag", [P, 1], I32)
        g_src = sb("g_src", [P, CAP], I32)
        g_dst = sb("g_dst", [P, CAP], I32)
        g_w = sb("g_w", [P, CAP])
        s_int = sb("s_int", [P, 2, CAP], I32)
        d8 = sb("d8", [P, CAP])
        w_rest = sb("w_rest", [P, 2, CAP])
        edge5 = sb("edge5", [P, 5, CAP], BF16)
        S_LO, KEY, W_HI, W_MID, W_LO = range(5)
        pairs = sb("pairs", [P, 5, NW * CH, 2], BF16)
        oh_lo = sb("oh_lo", [P, 2, HC, P], BF16)
        oh_key = sb("oh_key", [P, 2, HC, KEYS], BF16)
        wkey = sb("wkey", [P, 2, 3, HC, KEYS], BF16)
        at = sb("at", [P, 2, MT, P])
        c_part = sb("c_part", [P, NG, MT])
        c_sum = sb("c_sum", [P, MT])
        xn = sb("xn", [P, MT, D])
        stats = sb("stats", [P, MT, 6])
        mv = sb("mv", [P, MT, 2])
        std = sb("std", [P, MT])
        rstd = sb("rstd", [P, MT])
        ntn = sb("ntn", [P, 2, MT])
        negm = sb("negm", [P, MT])
        h0 = sb("h0", [P, 2, D])
        h0t = sb("h0t", [P, 2, D])
        sup = sb("sup", [P, MT, D])
        w_sb = {k: sb(f"w_{k}", [P, FT, D]) for k in ("W0", "W1", "gW1", "gW2", "gW3", "gWs")}
        b_sb = {k: sb(f"b_{k}", [1, D]) for k in ("b0", "b1", "gb1", "gb2", "gb3", "gbs")}
        h1 = sb("h1", [P, MT, D])
        u_sb = sb("u_sb", [P, FT])
        g_sb = sb("g_sb", [P, FT])
        z_sb = sb("z_sb", [P, 2, FT])
        rep = sb("rep", [P, 2, FT, P])
        row_s = sb("row_s", [P, D])
        row = sb("row", [P, D])
        gen_words = below[:, :, :, :].rearrange("p a b t -> p (a b t)")
        gen_int = gen_words[:, 0:4 * EP].bitcast(I32).rearrange("p (a e) -> p a e", a=2)
        gen_lo = gen_words[:, 4 * EP:6 * EP].bitcast(F32)
        gen_key = gen_words[:, 6 * EP:8 * EP].bitcast(F32)
        gen_oh = oh_lo[:, 0, 0:2, :].rearrange("p c k -> p (c k)").bitcast(F32)
        gen_rhs = wkey[:, 0, 0, 0:16, :].rearrange("p c k -> p (c k)").bitcast(F32)
        c_junk = h0[:, :, :].rearrange("p m (a d) -> p (m a) d", d=P)
        V_TILES = range(MT)
        EDGE_AT = 2

        ps_a = ps("ps_a", [P, 2, 2, 512])
        ps_g = ps("ps_g", [P, 2, 512])
        ps_m = ps("ps_m", [P, 2, 512])

        s_dst, s_srcw, s_x, s_w0, s_wts = sem("s_dst"), sem("s_srcw"), [sem(f"s_x{k}") for k in range(MT // 2)], sem("s_w0"), sem("s_wts")
        s_const, s_ident, s_iota_key = sem("s_const"), sem("s_ident"), sem("s_iota_key")
        s_below, s_cnt, s_ok, s_okcnt, s_start = (sem("s_below"), sem("s_cnt"), sem("s_ok"), sem("s_okcnt"),
                                                  sem("s_start"))
        s_gsd, s_gw = sem("s_gsd"), sem("s_gw")
        s_edge, s_etr, s_pairs = sem("s_edge"), sem("s_etr"), sem("s_pairs")
        s_onehot, s_wk, s_built, s_at, s_csum = (sem("s_onehot"), sem("s_wk"), sem("s_built"), sem("s_at"),
                                                   sem("s_csum"))
        s_var, s_std, s_rstd, s_h0, s_h0tp, s_h0t, s_supp, s_sup = (
            sem("s_var"), sem("s_std"), sem("s_rstd"), sem("s_h0"), sem("s_h0tp"), sem("s_h0t"), sem("s_supp"),
            sem("s_sup"))
        s_agg, s_h1 = sem("s_agg"), sem("s_h1")
        s_c, s_vec, s_vsb, s_sig, s_rep, s_rowp, s_rows, s_row, s_y, s_out = (
            sem("s_c"), sem("s_vec"), sem("s_vsb"), sem("s_sig"), sem("s_rep"), sem("s_rowp"), sem("s_rows"),
            sem("s_row"), sem("s_y"), sem("s_out"))
        s_gen_f, s_gen_mm, s_gen_key, s_gen_v = sem("s_gen_f"), sem("s_gen_mm"), sem("s_gen_key"), sem("s_gen_v")
        s_v, s_v2 = sem("s_v"), sem("s_v2")

        block = ctx.enter_context(nc.Block())

        @block.sync
        def _(sp):
            sp.dma_start(dst_flat[:, :], dst.rearrange("(p e) -> p e", p=P)).then_inc(s_dst, 16)
            xv = x.rearrange("(m p) d -> p m d", p=P)
            sp.dma_start(xn[:, 0:2, :], xv[:, 0:2, :]).then_inc(s_x[0], 16)
            sp.dma_start(w_sb["W0"][:, :, :], W0.rearrange("(f p) d -> p f d", p=P)).then_inc(s_w0, 16)
            for m in range(2, MT, 2):
                sp.dma_start(xn[:, m:m + 2, :], xv[:, m:m + 2, :]).then_inc(s_x[m // 2], 16)
            sp.dma_start(src_flat[:, :], src.rearrange("(p e) -> p e", p=P)).then_inc(s_srcw, 16)
            sp.dma_start(w_flat[:, :], edge_weight.rearrange("(p e) -> p e", p=P)).then_inc(s_srcw, 16)
            for k, v in (("b0", b0), ("b1", b1), ("gb1", gb1), ("gb2", gb2), ("gb3", gb3), ("gbs", gbs)):
                sp.dma_start(b_sb[k][:, :], v.rearrange("(a d) -> a d", a=1)).then_inc(s_wts, 16)
            for k, v in (("W1", W1), ("gW1", gW1), ("gW2", gW2), ("gW3", gW3), ("gWs", gWs)):
                sp.dma_start(w_sb[k][:, :, :], v.rearrange("(f p) d -> p f d", p=P)).then_inc(s_wts, 16)
            ov = out.rearrange("(m p) d -> p m d", p=P)
            for m in range(MT):
                sp.wait_ge(s_y, m + 1)
                sp.dma_start(ov[:, m, :], xn[:, m, :]).then_inc(s_out, 16)
            sp.wait_ge(s_out, 16 * MT)

        NCONST = 7

        @block.gpsimd
        def _(pool):
            pool.iota(iota_8t[:, :], [[WIN, P]], base=0, channel_multiplier=0,
                      allow_small_or_imprecise_dtypes=True).then_inc(s_const, 1)
            pool.memset(blk_cols[:, :, 0], 1.0).then_inc(s_const, 1)
            pool.iota(blk_cols[:, :, 1], [[0, NB]], base=0, channel_multiplier=1,
                      allow_small_or_imprecise_dtypes=True).then_inc(s_const, 1)
            pool.iota(blk_cols[:, :, 2], [[1, NB]], base=0, channel_multiplier=0,
                      allow_small_or_imprecise_dtypes=True).then_inc(s_const, 1)
            pool.memset(ones_bf[:, :], 1.0).then_inc(s_const, 1)
            pool.iota(win_base[:, :], [[0, 1]], base=0, channel_multiplier=WIN,
                      allow_small_or_imprecise_dtypes=True).then_inc(s_const, 1)
            pool.iota(iota_bf[:, :], [[1, P]], base=0, channel_multiplier=0,
                      allow_small_or_imprecise_dtypes=True).then_inc(s_const, 1)
            pool.memset(ident[:, :], 0.0).then_inc(s_ident, 1)
            pool.memset(ident_bf[:, :], 0.0).then_inc(s_ident, 1)
            pool.memset(ones_row[:, :], 1.0).then_inc(s_ident, 1)
            pool.memset(node_count[:, :], float(N)).then_inc(s_ident, 1)
            pool.wait_ge(s_ident, 4)
            for m in (ident, ident_bf):
                pool.affine_select(out=m[:, :], in_=m[:, :], compare_op=ALU.not_equal, fill=1.0, base=0,
                                   pattern=[[-1, P]], channel_multiplier=1).then_inc(s_ident, 1)
            pool.wait_ge(s_start, 2)
            for g, v, s in ((g_src, src, s_gsd), (g_dst, dst, s_gsd), (g_w, edge_weight, s_gw)):
                pool.indirect_dma_start(g[:, :], None, v.rearrange("(e one) -> e one", one=1),
                                        bass.IndirectOffsetOnAxis(ap=start[:, :], axis=0)).then_inc(s, 16)
            pool.iota(iota_key[:, :], [[1, 512]], base=0, channel_multiplier=0,
                      allow_small_or_imprecise_dtypes=True).then_inc(s_iota_key, 1)

        @block.vector
        def _(dve):
            v = nc.vector
            chain = [0]

            def link(ins):
                chain[0] += 1
                ins.then_inc(s_v, 1)
                dve.wait_ge(s_v, chain[0])

            dve.wait_ge(s_dst, 16)
            blocks = dst_flat[:, :].rearrange("p (b e) -> p b e", e=BLK)
            v.tensor_reduce(blk_max[:, :], blocks, AX_X, ALU.max)
            link(v.tensor_reduce(blk_min[:, :], blocks, AX_X, ALU.min))
            link(v.tensor_scalar(blk_min[:, :], blk_min[:, :], float(WIN - 1), None, ALU.subtract))
            dve.wait_ge(s_const, NCONST)
            for b in range(NB):
                v.tensor_scalar(below[:, 0, b, :], iota_8t[:, :], blk_max[:, b:b + 1], None,
                                ALU.is_gt).then_inc(s_below, 1)
                v.tensor_scalar(below[:, 1, b, :], iota_8t[:, :], blk_min[:, b:b + 1], None,
                                ALU.is_ge).then_inc(s_below, 1)
            dve.wait_ge(s_cnt, 1)
            link(v.tensor_copy(cnt[:, :, :], ps_m[:, 0, 0:6].rearrange("p (a b) -> p a b", a=2)))
            n_blk = cnt[:, :, 0]
            idx_sum, twice, good = chk[:, 0:2], chk[:, 2:4], chk[:, 4:6]
            v.scalar_tensor_tensor(idx_sum, cnt[:, :, 1], float(NB), cnt[:, :, 2], ALU.mult, ALU.add)
            link(v.scalar_tensor_tensor(twice, n_blk, 1.0, n_blk, ALU.subtract, ALU.mult))
            link(v.scalar_tensor_tensor(good, idx_sum, 2.0, twice, ALU.mult, ALU.is_equal))
            link(v.tensor_tensor(chk[:, 6:7], cnt[:, 1, 0:1], cnt[:, 0, 0:1], ALU.subtract))
            link(v.scalar_tensor_tensor(chk[:, 7:8], chk[:, 6:7], float(CAP // BLK), chk[:, 4:5], ALU.is_le, ALU.mult))
            v.tensor_tensor(in_order[:, :], chk[:, 7:8], chk[:, 5:6], ALU.mult).then_inc(s_ok, 1)
            link(v.tensor_scalar(chk[:, 8:9], cnt[:, 0, 0:1], float(BLK), float(E - CAP), ALU.mult, ALU.min))
            dve.wait_ge(s_okcnt, 1)
            link(v.tensor_scalar(chk[:, 9:10], ps_m[:, 1, 0:1], float(NW), None, ALU.is_ge))
            v.tensor_tensor(start[:, :], chk[:, 8:9], chk[:, 9:10], ALU.mult).then_inc(s_start, 1)
            v.tensor_copy(flag[:, :], chk[:, 9:10]).then_inc(s_start, 1)

            for m in range(MT):
                if m % 2 == 0:
                    dve.wait_ge(s_x[m // 2], 16)
                v.bn_stats(stats[:, m, :], xn[:, m, :]).then_inc(s_v, 1)
                chain[0] += 1
            dve.wait_ge(s_v, chain[0])
            for m in range(MT):
                ins = v.bn_aggr(mv[:, m, :], stats[:, m, :])
            link(ins)
            link(v.tensor_scalar(ntn[:, 0, :], mv[:, :, 1], EPS, None, ALU.add))
            v.tensor_copy(ntn[:, 1, :], ntn[:, 0, :]).then_inc(s_var, 1)
            dve.wait_ge(s_std, 1)
            link(v.reciprocal(rstd[:, :], std[:, :]))
            link(v.tensor_tensor(ntn[:, 1, :], rstd[:, :], rstd[:, :], ALU.mult))
            link(v.tensor_tensor(ntn[:, 1, :], ntn[:, 1, :], ntn[:, 0, :], ALU.mult))
            link(v.tensor_scalar(ntn[:, 1, :], ntn[:, 1, :], -0.5, 1.5, ALU.mult, ALU.add))
            link(v.tensor_tensor(rstd[:, :], rstd[:, :], ntn[:, 1, :], ALU.mult))
            v.scalar_tensor_tensor(negm[:, :], mv[:, :, 0], -1.0, rstd[:, :], ALU.mult, ALU.mult).then_inc(s_rstd, 1)

            dve.wait_ge(s_gsd, 32)
            v.tensor_scalar(s_int[:, 0, :], g_src[:, :], P - 1, None, ALU.bitwise_and)
            v.tensor_scalar(s_int[:, 1, :], g_src[:, :], 7, None, ALU.logical_shift_right)
            link(v.tensor_scalar(d8[:, :], g_dst[:, :], win_base[:, :], float(MT), ALU.subtract, ALU.mult))
            v.tensor_copy(edge5[:, S_LO, :], s_int[:, 0, :]).then_inc(s_edge, 1)
            v.tensor_tensor(edge5[:, KEY, :], d8[:, :], s_int[:, 1, :], ALU.add).then_inc(s_edge, 1)
            dve.wait_ge(s_gw, 16)
            v.tensor_copy(edge5[:, W_HI, :], g_w[:, :]).then_inc(s_edge, 1)
            dve.wait_ge(s_edge, 3)
            link(v.tensor_tensor(w_rest[:, 0, :], g_w[:, :], edge5[:, W_HI, :], ALU.subtract))
            v.tensor_copy(edge5[:, W_MID, :], w_rest[:, 0, :]).then_inc(s_edge, 1)
            dve.wait_ge(s_edge, 4)
            link(v.tensor_tensor(w_rest[:, 1, :], w_rest[:, 0, :], edge5[:, W_MID, :], ALU.subtract))
            v.tensor_copy(edge5[:, W_LO, :], w_rest[:, 1, :]).then_inc(s_edge, 1)

            def factors(h, b, reused):
                cols = pairs[:, :, bass.ds(h * HC, HC), :]
                if reused:
                    dve.wait_ge(s_built, h - 1)
                v.tensor_tensor(oh_lo[:, b].rearrange("p c (k two) -> p c k two", two=2),
                                iota_bf[:, :].rearrange("p (k two) -> p k two", two=2)
                                .unsqueeze(1).broadcast_to([P, HC, P // 2, 2]),
                                cols[:, S_LO].unsqueeze(2).broadcast_to([P, HC, P // 2, 2]),
                                ALU.is_equal).then_inc(s_onehot, 1)
                v.tensor_tensor(oh_key[:, b].rearrange("p c (k two) -> p c k two", two=2),
                                iota_bf[:, 0:KEYS].rearrange("p (k two) -> p k two", two=2)
                                .unsqueeze(1).broadcast_to([P, HC, KEYS // 2, 2]),
                                cols[:, KEY].unsqueeze(2).broadcast_to([P, HC, KEYS // 2, 2]),
                                ALU.is_equal).then_inc(s_onehot, 1)
                dve.wait_ge(s_onehot, 2 * h + 2)
                for part in range(3):
                    v.tensor_tensor(wkey[:, b, part].rearrange("p c (k two) -> p c k two", two=2),
                                    oh_key[:, b].rearrange("p c (k two) -> p c k two", two=2),
                                    cols[:, W_HI + part].unsqueeze(2).broadcast_to([P, HC, KEYS // 2, 2]),
                                    ALU.mult).then_inc(s_wk, 1)

            def general_factors(h):
                with dve.Fori(0, EP) as e:
                    step = h * EP + e
                    dve.wait_ge(s_gen_mm, step + 1)
                    v.tensor_scalar(gen_oh, iota_bf[:, :], gen_lo[:, bass.ds(e, 1)], None,
                                    ALU.is_equal).then_inc(s_gen_f, 1)
                    dve.wait_ge(s_gen_key, h + 1)
                    v.tensor_scalar(gen_rhs, iota_key[:, :], gen_key[:, bass.ds(e, 1)], w_flat[:, bass.ds(e, 1)],
                                    ALU.is_equal, ALU.mult).then_inc(s_gen_f, 1)
                dve.wait_ge(s_gen_f, 2 * (h + 1) * EP)
                v.tensor_scalar(gen_key, gen_key, -512.0, None, ALU.add).then_inc(s_gen_key, 1)

            dve.wait_ge(s_start, 2)
            order_reg = dve.value_load(flag[0:1, 0:1], min_val=0, max_val=1)
            dve.wait_ge(s_pairs, 5)
            with dve.If(order_reg == 1):
                factors(0, 0, False)
                factors(1, 1, False)
                with dve.Fori(1, NG) as i:
                    factors(2 * i, 0, True)
                    factors(2 * i + 1, 1, True)
            with dve.Else():
                dve.wait_ge(s_srcw, 32)
                dve.wait_ge(s_iota_key, 1)
                v.tensor_scalar(gen_int[:, 0, :], src_flat[:, :], P - 1, None, ALU.bitwise_and).then_inc(s_gen_v, 1)
                v.tensor_scalar(gen_int[:, 1, :], src_flat[:, :], 7, None,
                                ALU.logical_shift_right).then_inc(s_gen_v, 1)
                dve.wait_ge(s_gen_v, 2)
                v.tensor_copy(gen_lo, gen_int[:, 0, :]).then_inc(s_gen_v, 1)
                v.scalar_tensor_tensor(gen_key, dst_flat[:, :], float(MT), gen_int[:, 1, :],
                                       ALU.mult, ALU.add).then_inc(s_gen_key, 1)
                dve.wait_ge(s_gen_v, 3)
                with dve.Fori(0, NH) as h:
                    general_factors(h)

            def link2(ins, n):
                ins.then_inc(s_v2, 1)
                dve.wait_ge(s_v2, n)

            dve.wait_ge(s_c, NG * MT)
            v.tensor_reduce(c_sum[:, :], c_part[:, :, :].rearrange("p g s -> p s g"), AX_X,
                            ALU.add).then_inc(s_csum, 1)
            dve.wait_ge(s_vec, 1)
            v.tensor_copy(u_sb[:, :], ps_m[:, 0, 0:FT]).then_inc(s_vsb, 1)
            dve.wait_ge(s_sig, 1)
            v.tensor_copy(rep[:, 0], g_sb[:, :].unsqueeze(2).broadcast_to([P, FT, P])).then_inc(s_rep, 1)
            dve.wait_ge(s_vec, 3)
            v.tensor_scalar(z_sb[:, 0, :], ps_m[:, 0, 0:FT], 0.0, None, ALU.max).then_inc(s_vsb, 1)
            dve.wait_ge(s_vec, 4)
            link2(v.tensor_scalar(z_sb[:, 1, :], ps_m[:, 1, 0:FT], 0.0, None, ALU.max), 1)
            v.tensor_copy(rep[:, 1], z_sb[:, 1, :].unsqueeze(2).broadcast_to([P, FT, P])).then_inc(s_rep, 1)
            dve.wait_ge(s_rowp, 2)
            dve.wait_ge(s_rows, 1)
            v.scalar_tensor_tensor(row[:, :], ps_a[:, 1, 0, :], 0.0, row_s[:, :], ALU.max,
                                   ALU.add).then_inc(s_row, 1)
            dve.wait_ge(s_row, 1)
            for m in V_TILES:
                v.tensor_tensor(xn[:, m, :], xn[:, m, :], row[:, :], ALU.add).then_inc(s_y, 1)

        @block.scalar
        def _(act):
            a = nc.scalar
            act.wait_ge(s_var, 1)
            a.activation(std[:, :], ntn[:, 1, :], ACT.Sqrt).then_inc(s_std, 1)
            act.wait_ge(s_rstd, 1)

            def normalise(m):
                if m >= 2:
                    act.wait_ge(s_h0tp, m - 1)
                a.activation(h0[:, m % 2, :], xn[:, m, :], ACT.Relu, bias=negm[:, m:m + 1],
                             scale=rstd[:, m:m + 1]).then_inc(s_h0, 1)

            def edge_values(r):
                act.wait_ge(s_etr, min(r + 2 - r % 2, 5))
                half = ps_a[:, r // 4, r // 2 % 2, :].bitcast(BF16)[:, r % 2 * CAP:r % 2 * CAP + CAP]
                a.activation(pairs[:, r].rearrange("p (w c) two -> p w c two", c=CH),
                             half.rearrange("p (c w) -> p w c", c=CH).unsqueeze(3).broadcast_to([P, NW, CH, 2]),
                             ACT.Copy).then_inc(s_pairs, 1)

            def support_out(m):
                act.wait_ge(s_supp, m + 1)
                a.activation(sup[:, m, :], ps_g[:, m % 2, :], ACT.Copy).then_inc(s_sup, 1)

            normalise(0)
            normalise(1)
            for m in range(MT):
                act.wait_ge(s_h0tp, m + 1)
                if m >= 2:
                    act.wait_ge(s_supp, m - 1)
                a.activation(h0t[:, m % 2, :], ps_m[:, m % 2, :], ACT.Copy).then_inc(s_h0t, 1)
                if m + 2 < MT:
                    normalise(m + 2)
                if m >= 1:
                    support_out(m - 1)
                if m == EDGE_AT:
                    for r in range(5):
                        edge_values(r)
            support_out(MT - 1)

            def at_out(h, par, b, i, reused):
                act.wait_ge(s_built, h + 1)
                if reused and b == 0:
                    act.wait_ge(s_agg, i - 1)
                a.activation(at[:, par, :, b * HD:(b + 1) * HD].rearrange("p s d -> p d s"),
                             ps_a[:, par, b, :].rearrange("p (d s) -> p d s", s=MT), ACT.Copy).then_inc(s_at, 1)

            def column_sums(i, par):
                act.wait_ge(s_at, 2 * i + 2)
                act.wait_ge(s_c, MT * i)
                for s in range(MT):
                    a.activation(c_junk[:, s, :], at[:, par, s, :], ACT.Copy,
                                 accum_out=c_part[:, bass.ds(i, 1), s]).then_inc(s_c, 1)

            def h1_out(i, par):
                act.wait_ge(s_agg, i + 1)
                a.activation(h1[:, bass.ds(i, 1), :], ps_g[:, par:par + 1, :], ACT.Relu).then_inc(s_h1, 1)

            for b in range(2):
                at_out(b, 0, b, 0, False)
            column_sums(0, 0)
            for b in range(2):
                at_out(2 + b, 1, b, 1, False)
            column_sums(1, 1)
            h1_out(0, 0)
            with act.Fori(1, NG // 2) as p:
                for par in range(2):
                    i = 2 * p + par
                    for b in range(2):
                        at_out(2 * i + b, par, b, i, True)
                    column_sums(i, par)
                    h1_out(i - 1, 1 - par)
            h1_out(NG - 1, 1)

            act.wait_ge(s_vec, 2)
            a.activation(g_sb[:, :], ps_m[:, 1, 0:FT], ACT.Sigmoid, scale=1.0 / N).then_inc(s_sig, 1)
            act.wait_ge(s_rowp, 1)
            a.activation(row_s[:, :], ps_a[:, 0, 0, :], ACT.Copy).then_inc(s_rows, 1)

        @block.tensor
        def _(pe):
            mm = nc.tensor.matmul
            pe.wait_ge(s_const, NCONST)
            for b in range(NB):
                pe.wait_ge(s_below, 2 * b + 1)
                last = mm(ps_m[:, 0, 0:3], below[:, 0, b, :], blk_cols[:, b, :], start=b == 0, stop=b == NB - 1)
            pe.wait_ge(s_below, 2 * NB)
            for b in range(NB):
                last = mm(ps_m[:, 0, 3:6], below[:, 1, b, :], blk_cols[:, b, :], start=b == 0, stop=b == NB - 1)
            last.then_inc(s_cnt, 1)
            pe.wait_ge(s_ok, 1)
            mm(ps_m[:, 1, 0:1], ones_bf[:, :], in_order[:, :], start=True, stop=True).then_inc(s_okcnt, 1)

            def transpose_h0(m):
                pe.wait_ge(s_h0, m + 1)
                if m >= 2:
                    pe.wait_ge(s_h0t, m - 1)
                for f in range(FT):
                    last = nc.tensor.transpose(ps_m[:, m % 2, f * P:(f + 1) * P], h0[:, m % 2, f * P:(f + 1) * P],
                                               ident[:, :])
                last.then_inc(s_h0tp, 1)

            def transpose_edges(r):
                pe.wait_ge(s_edge, r + 1)
                half = ps_a[:, r // 4, r // 2 % 2, :].bitcast(BF16)
                for c in range(CH):
                    o = r % 2 * CAP + c * P
                    last = nc.tensor.transpose(half[:, o:o + P], edge5[:, r, c * P:(c + 1) * P], ident_bf[:, :])
                last.then_inc(s_etr, 1)

            pe.wait_ge(s_ident, 6)
            pe.wait_ge(s_start, 2)
            transpose_h0(0)
            for m in range(MT):
                if m + 1 < MT:
                    transpose_h0(m + 1)
                if m == 0:
                    pe.wait_ge(s_w0, 16)
                pe.wait_ge(s_h0t, m + 1)
                if m >= 2:
                    pe.wait_ge(s_sup, m - 1)
                for f in range(FT):
                    last = mm(ps_g[:, m % 2, :], h0t[:, m % 2, f * P:(f + 1) * P], w_sb["W0"][:, f, :],
                              start=f == 0, stop=f == FT - 1)
                last.then_inc(s_supp, 1)
                if m == EDGE_AT - 1:
                    for r in range(5):
                        transpose_edges(r)

            def build(h, par, b, i, reused):
                pe.wait_ge(s_onehot, 2 * h + 2)
                pe.wait_ge(s_wk, 3 * h + 3)
                if reused:
                    pe.wait_ge(s_at, h - 3)
                for wdw in range(HC // CH):
                    for c in range(CH):
                        for part in range(3):
                            last = mm(ps_a[:, par, b, wdw * KEYS:(wdw + 1) * KEYS], oh_lo[:, b, wdw * CH + c, :],
                                      wkey[:, b, part, wdw * CH + c, :], start=c == 0 and part == 0,
                                      stop=c == CH - 1 and part == 2)
                last.then_inc(s_built, 1)

            def aggregate(i, par, reused):
                pe.wait_ge(s_at, 2 * i + 2)
                if reused:
                    pe.wait_ge(s_h1, i - 1)
                mm(ps_g[:, par, :], ones_row[:, :], b_sb["b0"][:, :], start=True, stop=False)
                for s in range(MT):
                    last = mm(ps_g[:, par, :], at[:, par, s, :], sup[:, s, :], start=False, stop=s == MT - 1)
                last.then_inc(s_agg, 1)

            def general_build(h, par, b, reused):
                if reused:
                    pe.wait_ge(s_at, h - 3)
                pe.wait_ge(s_gen_f, 2 * h * EP + 2)
                mm(ps_a[:, par, b, :], gen_oh, gen_rhs, start=True, stop=False,
                   skip_group_check=True).then_inc(s_gen_mm, 1)
                with pe.Fori(1, EP) as e:
                    pe.wait_ge(s_gen_f, 2 * h * EP + 2 * e + 2)
                    mm(ps_a[:, par, b, :], gen_oh, gen_rhs, start=False, stop=True,
                       skip_group_check=True).then_inc(s_gen_mm, 1)
                pe.wait_ge(s_gen_mm, (h + 1) * EP + 1)
                pe.sem_inc(s_built, 1)

            pe.wait_ge(s_wts, 16 * 11)
            pe.wait_ge(s_sup, MT)
            pe.wait_ge(s_pairs, 5)
            order_reg = pe.value_load(flag[0:1, 0:1], min_val=0, max_val=1)
            with pe.If(order_reg == 1):
                for h in range(4):
                    build(h, h // 2, h % 2, h // 2, False)
                aggregate(0, 0, False)
                build(4, 0, 0, 2, True)
                build(5, 0, 1, 2, True)
                aggregate(1, 1, False)
                with pe.Fori(1, NG // 2 - 1) as p:
                    for par in range(2):
                        i = 2 * p + par
                        for b in range(2):
                            build(2 * (i + 1) + b, 1 - par, b, i + 1, True)
                        aggregate(i, par, True)
                for b in range(2):
                    build(2 * (NG - 1) + b, 1, b, NG - 1, True)
                aggregate(NG - 2, 0, True)
                aggregate(NG - 1, 1, True)
            with pe.Else():
                pe.sem_inc(s_gen_mm, 1)
                for i in range(2):
                    for b in range(2):
                        general_build(2 * i + b, i, b, False)
                    aggregate(i, i, False)
                with pe.Fori(1, NG // 2) as p:
                    for par in range(2):
                        i = 2 * p + par
                        for b in range(2):
                            general_build(2 * i + b, par, b, True)
                        aggregate(i, par, True)

            def vector_layer(o, vec, wt, bias, bias_scale, sem_in, n):
                for q in range(FT):
                    mm(o[:, q:q + 1], bias[:, q * P:(q + 1) * P], bias_scale, start=True, stop=False)
                    if q == 0:
                        pe.wait_ge(sem_in, n)
                    for f in range(FT):
                        last = mm(o[:, q:q + 1], wt[:, f, q * P:(q + 1) * P], vec[:, f:f + 1], start=False,
                                  stop=f == FT - 1)
                last.then_inc(s_vec, 1)

            def row_layer(o, lhs, wt, bias):
                mm(o, ones_row[:, :], bias[:, :], start=True, stop=False)
                for f in range(FT):
                    last = mm(o, lhs[:, f, :], wt[:, f, :], start=False, stop=f == FT - 1)
                last.then_inc(s_rowp, 1)

            pe.wait_ge(s_csum, 1)
            pe.wait_ge(s_h1, NG)
            for q in range(FT):
                for i in range(MT):
                    last = mm(ps_m[:, 0, q:q + 1], h1[:, i, q * P:(q + 1) * P], c_sum[:, i:i + 1], start=i == 0,
                              stop=i == MT - 1)
            last.then_inc(s_vec, 1)
            one = ones_row[:, 0:1]
            vector_layer(ps_m[:, 1, 0:FT], u_sb, w_sb["W1"], b_sb["b1"], node_count[:, :], s_vsb, 1)
            vector_layer(ps_m[:, 0, 0:FT], g_sb, w_sb["gW1"], b_sb["gb1"], one, s_sig, 1)
            vector_layer(ps_m[:, 1, 0:FT], z_sb[:, 0, :], w_sb["gW2"], b_sb["gb2"], one, s_vsb, 2)
            pe.wait_ge(s_rep, 1)
            row_layer(ps_a[:, 0, 0, :], rep[:, 0], w_sb["gWs"], b_sb["gbs"])
            pe.wait_ge(s_rep, 2)
            row_layer(ps_a[:, 1, 0, :], rep[:, 1], w_sb["gW3"], b_sb["gb3"])


_INS = ['x', 'src', 'dst', 'edge_weight', 'L0_gnn_W0', 'L0_gnn_b0', 'L0_gnn_W1', 'L0_gnn_b1', 'L0_gnn_gW1',
        'L0_gnn_gb1', 'L0_gnn_gW2', 'L0_gnn_gb2', 'L0_gnn_gW3', 'L0_gnn_gb3', 'L0_gnn_gWs', 'L0_gnn_gbs']
_OUTS = [((1024, 512), 'float32')]


def kernel(**inputs):
    import numpy as _np
    import concourse.bacc as _bacc
    from concourse import mybir as _mybir
    from concourse.bass_utils import run_bass_kernel_spmd as _run

    nc = _bacc.Bacc("TRN2", target_bir_lowering=False, num_devices=1)
    arrays, args = {}, []
    for name in _INS:
        a = _np.ascontiguousarray(inputs[name])
        arrays[f"in_{name}_dram"] = a
        args.append(nc.dram_tensor(f"in_{name}_dram", a.shape, _mybir.dt.from_np(a.dtype), kind="ExternalInput").ap())
    for i, (shape, dtype) in enumerate(_OUTS):
        dt = _mybir.dt.from_np(_np.dtype(dtype))
        args.append(nc.dram_tensor(f"out_{i}_dram", shape, dt, kind="ExternalOutput").ap())
    gnn_block(nc, *args)
    r = _run(nc, [arrays], core_ids=[0])
    return r.results[0]["out_0_dram"]
```

```python
import concourse.bass as bass
from concourse import mybir
from contextlib import ExitStack

F32 = mybir.dt.float32
BF16 = mybir.dt.bfloat16
I32 = mybir.dt.int32
U32 = mybir.dt.uint32
ALU = mybir.AluOpType
ACT = mybir.ActivationFunctionType
AX_X = mybir.AxisListType.X

F16 = mybir.dt.float16
F32R = mybir.dt.float32r
P = 128


def gnn_block(nc, x, src, dst, edge_weight, W0, b0, W1, b1, gW1, gb1, gW2, gb2, gW3, gb3, gWs, gbs, out):
    N, D = x.shape
    E = src.shape[0]
    MT = N // P
    FT = D // P
    WIN = 8
    NW = N // WIN
    CH = 3
    CAP = CH * P
    KEYS = WIN * MT
    NG = N // P
    NH = 2 * NG
    HD = P // 2
    HC = HD // WIN * CH
    EP = E // P
    BLK = 24
    NB = EP // BLK
    Q = P // FT
    EPS = 1e-5
    TOP = 2.0 ** 14
    TINY = 2.0 ** -100
    LOW_AFTER = {1: [0], 2: [1], 3: [2], 4: [3], 5: [], 6: [], 7: [4, 5], 8: [], 9: [6, 7], 10: [8], 11: [9],
                 12: [10], 13: [11], 14: [12, 13], 15: [], 16: [14, 15]}
    PE_ORDER = [("product", 0), ("build", 6), ("build", 7), ("product", 1), ("build", 8), ("product", 2),
                ("build", 9), ("product", 3), ("build", 10), ("build", 11), ("product", 4), ("build", 12),
                ("build", 13), ("product", 5), ("build", 14), ("build", 15), ("product", 6), ("product", 7)]
    assert NW == P and KEYS * (HD // WIN) == 512 and EP % BLK == 0 and CAP % BLK == 0 and NG == MT == 8

    ctx = ExitStack()
    with ctx:
        def sb(name, shape, dt=F32):
            return ctx.enter_context(nc.sbuf_tensor(name, shape, dt))

        def ps(name, shape, dt=F32):
            return ctx.enter_context(nc.psum_tensor(name, shape, dt))

        def sem(name):
            return ctx.enter_context(nc.semaphore(name))

        iota_16 = sb("iota_16", [P, P], F16)
        iota_key = sb("iota_key", [P, 512])
        win_base = sb("win_base", [P, 1])
        ident_16 = sb("ident_16", [P, P], F16)
        ident = sb("ident", [P, P])
        ones_16 = sb("ones_16", [P, P], F16)
        ones_32 = sb("ones_32", [P, P])
        ones_r = sb("ones_r", [2, P], F32R)
        sel = sb("sel", [P, P])
        node_count = sb("node_count", [1, 1])
        blk_cols = sb("blk_cols", [P, NB, 3], F16)
        row_id = sb("row_id", [2, 2])
        dst_flat = sb("dst_flat", [P, EP], I32)
        src_flat = sb("src_flat", [P, EP], I32)
        w_flat = sb("w_flat", [P, EP])
        blk = sb("blk", [P, 2, 2, NB], I32)
        blk2 = sb("blk2", [P, 2, NB, 2], F16)
        below = sb("below", [P, 2, NB, P], F16)
        cnt = sb("cnt", [P, 2, 3])
        chk = sb("chk", [P, 16])
        in_order = sb("in_order", [P, 1], F16)
        start = sb("start", [P, 1], U32)
        flag = sb("flag", [P, 1], I32)
        w_top = sb("w_top", [P, 4])
        w_diag = sb("w_diag", [P, P])
        w_scale = sb("w_scale", [P, 1])
        w_unscale = sb("w_unscale", [P, 1])
        S_LO, KEY, W_HI, W_LO = range(4)
        pairs = sb("pairs", [P, 4, NW * CH, 2], F16)
        oh_lo = sb("oh_lo", [P, 2, HC, P], F16)
        oh_key = sb("oh_key", [P, 2, HC, KEYS], F16)
        wkey = sb("wkey", [P, 2, 2, HC, KEYS], F16)
        at_hi = sb("at_hi", [P, 2, MT, P], F32R)
        at_lo = sb("at_lo", [P, 2, MT, P], F32R)
        c_part = sb("c_part", [P, NG, MT])
        c_sum = sb("c_sum", [P, MT])
        c_junk = sb("c_junk", [P, MT, P], F16)
        xn = sb("xn", [P, MT, D])
        stats = sb("stats", [P, MT, 6])
        mv = sb("mv", [P, MT, 2])
        std = sb("std", [P, MT])
        rstd = sb("rstd", [P, MT])
        ntn = sb("ntn", [P, 2, MT])
        negm = sb("negm", [P, MT])
        h0 = sb("h0", [P, 2, D])
        h0t = sb("h0t", [P, 2, D])
        sup_hi = sb("sup_hi", [P, MT, D], F32R)
        sup_lo = sb("sup_lo", [P, MT, D], F32R)
        w_sb = {k: sb(f"w_{k}", [P, FT, D]) for k in ("W0", "W1", "gW1", "gW2", "gW3")}
        b_sb = {k: sb(f"b_{k}", [1, D]) for k in ("b1", "gb1", "gb2", "gb3", "gbs")}
        b0_sb = sb("b0_sb", [2, D])
        b0_r = sb("b0_r", [2, 2, D], F32R)
        b0_t = sb("b0_t", [2, 2, D])
        h1 = sb("h1", [P, MT, D])
        col = sb("col", [P, 4, FT])
        rep = sb("rep", [P, 4, FT, Q])

        words = wkey[:, :, :, :, :].rearrange("p a b c k -> p (a b c k)")
        g_src = words[:, 0:2 * CAP].bitcast(I32)
        g_dst = words[:, 2 * CAP:4 * CAP].bitcast(I32)
        g_w = words[:, 4 * CAP:6 * CAP].bitcast(F32)
        s_int = words[:, 6 * CAP:10 * CAP].bitcast(I32).rearrange("p (a e) -> p a e", a=2)
        d8 = words[:, 10 * CAP:12 * CAP].bitcast(F32)
        edge4 = words[:, 12 * CAP:16 * CAP].rearrange("p (a e) -> p a e", a=4)
        gen_words = below[:, :, :, :].rearrange("p a b t -> p (a b t)")
        gen_int = gen_words[:, 0:4 * EP].bitcast(I32).rearrange("p (a e) -> p a e", a=2)
        gen_lo = gen_words[:, 4 * EP:6 * EP].bitcast(F32)
        gen_key = gen_words[:, 6 * EP:8 * EP].bitcast(F32)
        gen_oh = oh_lo[:, 0, 0:2, :].rearrange("p c k -> p (c k)").bitcast(F32)
        gen_rhs = oh_lo[:, 1, 0:8, :].rearrange("p c k -> p (c k)").bitcast(F32)
        late = oh_lo[:, :, :, :].rearrange("p a c k -> p (a c k)").bitcast(F32)
        acc = late[:, 0:D]
        row_s = late[:, D:2 * D]
        row = late[:, 2 * D:3 * D]
        rows, rows_g = h0[:, 0, :], h0[:, 1, :]
        w_gWs = w_sb["W0"]

        ps_a = ps("ps_a", [P, 2, 2, 512])
        ps_g = ps("ps_g", [P, 2, 512])
        ps_m = ps("ps_m", [P, 2, 512])

        s_dst, s_wf, s_sf, s_w0, s_b0, s_wts, s_gws = (sem(k) for k in (
            "s_dst", "s_wf", "s_sf", "s_w0", "s_b0", "s_wts", "s_gws"))
        s_x = [sem(f"s_x{k}") for k in range(MT // 2)]
        s_const, s_ident, s_ones, s_b0p, s_b0r = (sem(k) for k in ("s_const", "s_ident", "s_ones", "s_b0p", "s_b0r"))
        s_below, s_diag, s_wrep, s_cnt, s_ok, s_okcnt, s_start = (sem(k) for k in (
            "s_below", "s_diag", "s_wrep", "s_cnt", "s_ok", "s_okcnt", "s_start"))
        s_gsd, s_gw, s_edge, s_etr, s_pairs = (sem(k) for k in ("s_gsd", "s_gw", "s_edge", "s_etr", "s_pairs"))
        s_onehot, s_wk, s_built, s_athi, s_atlo, s_c = (sem(k) for k in (
            "s_onehot", "s_wk", "s_built", "s_athi", "s_atlo", "s_c"))
        s_var, s_std, s_rstd, s_h0, s_h0tp, s_h0t, s_supp, s_suphi, s_suplo = (sem(k) for k in (
            "s_var", "s_std", "s_rstd", "s_h0", "s_h0tp", "s_h0t", "s_supp", "s_suphi", "s_suplo"))
        s_agg, s_h1, s_csum, s_acc = (sem(k) for k in ("s_agg", "s_h1", "s_csum", "s_acc"))
        s_colp, s_col, s_rep, s_rowp, s_rows, s_rowsg, s_finp, s_rowsum, s_row, s_y, s_out = (sem(k) for k in (
            "s_colp", "s_col", "s_rep", "s_rowp", "s_rows", "s_rowsg", "s_finp", "s_rowsum", "s_row", "s_y", "s_out"))
        s_gen_f, s_gen_mm, s_gen_key, s_gen_v = (sem(k) for k in ("s_gen_f", "s_gen_mm", "s_gen_key", "s_gen_v"))
        s_v = sem("s_v")

        block = ctx.enter_context(nc.Block())
        NCONST = 6

        @block.sync
        def _(sp):
            sp.dma_start(dst_flat[:, :], dst.rearrange("(p e) -> p e", p=P)).then_inc(s_dst, 16)
            sp.dma_start(w_flat[:, :], edge_weight.rearrange("(p e) -> p e", p=P)).then_inc(s_wf, 16)
            xv = x.rearrange("(m p) d -> p m d", p=P)
            for m in range(0, MT, 2):
                sp.dma_start(xn[:, m:m + 2, :], xv[:, m:m + 2, :]).then_inc(s_x[m // 2], 16)
            sp.dma_start(w_sb["W0"][:, :, :], W0.rearrange("(f p) d -> p f d", p=P)).then_inc(s_w0, 16)
            for r in range(2):
                sp.dma_start(b0_sb[r:r + 1, :], b0.rearrange("(a d) -> a d", a=1)).then_inc(s_b0, 16)
            sp.wait_ge(s_gsd, 32)
            sp.wait_ge(s_gw, 16)
            sp.dma_start(src_flat[:, :], src.rearrange("(p e) -> p e", p=P)).then_inc(s_sf, 16)
            for k, v in (("b1", b1), ("gb1", gb1), ("gb2", gb2), ("gb3", gb3), ("gbs", gbs)):
                sp.dma_start(b_sb[k][:, :], v.rearrange("(a d) -> a d", a=1)).then_inc(s_wts, 16)
            for k, v in (("W1", W1), ("gW1", gW1), ("gW2", gW2), ("gW3", gW3)):
                sp.dma_start(w_sb[k][:, :, :], v.rearrange("(f p) d -> p f d", p=P)).then_inc(s_wts, 16)
            sp.wait_ge(s_supp, MT)
            sp.dma_start(w_gWs[:, :, :], gWs.rearrange("(f p) d -> p f d", p=P)).then_inc(s_gws, 16)
            ov = out.rearrange("(m p) d -> p m d", p=P)
            for m in range(MT):
                sp.wait_ge(s_y, m + 1)
                sp.dma_start(ov[:, m, :], xn[:, m, :]).then_inc(s_out, 16)
            sp.wait_ge(s_out, 16 * MT)

        @block.gpsimd
        def _(pool):
            def iota(o, pattern, mult, s):
                pool.iota(o, pattern, base=0, channel_multiplier=mult,
                          allow_small_or_imprecise_dtypes=True).then_inc(s, 1)

            iota(iota_16[:, :], [[1, P]], 0, s_const)
            pool.memset(blk_cols[:, :, 0], 1.0).then_inc(s_const, 1)
            iota(blk_cols[:, :, 1], [[0, NB]], 1, s_const)
            iota(blk_cols[:, :, 2], [[1, NB]], 0, s_const)
            pool.memset(ones_16[:, :], 1.0).then_inc(s_const, 1)
            iota(win_base[:, :], [[0, 1]], WIN, s_const)
            pool.memset(ident[:, :], 0.0).then_inc(s_ident, 1)
            pool.memset(ones_32[:, :], 1.0).then_inc(s_ident, 1)
            pool.memset(ident_16[:, :], 0.0).then_inc(s_ident, 1)
            pool.wait_ge(s_ident, 3)
            for m in (ident, ident_16):
                pool.affine_select(out=m[:, :], in_=m[:, :], compare_op=ALU.not_equal, fill=1.0, base=0,
                                   pattern=[[-1, P]], channel_multiplier=1).then_inc(s_ident, 1)
            pool.memset(node_count[:, :], float(N)).then_inc(s_ones, 1)
            pool.memset(ones_r[:, :].bitcast(F32), 1.0).then_inc(s_ones, 1)
            pool.memset(sel[:, :], 0.0).then_inc(s_ones, 1)
            pool.wait_ge(s_ones, 3)
            for f in range(FT):
                pool.memset(sel[f * Q:f * Q + 1, :], 1.0).then_inc(s_ones, 1)
            iota(row_id[:, 0:1], [[0, 1]], 1, s_b0p)
            pool.wait_ge(s_b0p, 1)
            pool.tensor_scalar(row_id[:, 1:2], row_id[:, 0:1], -1.0, 1.0, ALU.mult, ALU.add).then_inc(s_b0p, 1)
            pool.wait_ge(s_start, 2)
            for g, v, s in ((g_src, src, s_gsd), (g_dst, dst, s_gsd), (g_w, edge_weight, s_gw)):
                pool.indirect_dma_start(g, None, v.rearrange("(e one) -> e one", one=1),
                                        bass.IndirectOffsetOnAxis(ap=start[:, :], axis=0)).then_inc(s, 16)
            pool.wait_ge(s_b0, 32)
            pool.wait_ge(s_b0r, 1)
            pool.tensor_tensor(b0_t[:, 0, :], b0_sb[:, :], b0_r[:, 0, :].bitcast(F32), ALU.subtract).then_inc(s_b0p, 1)
            pool.wait_ge(s_b0p, 3)
            pool.tensor_scalar(b0_t[:, 0, :], b0_t[:, 0, :], row_id[:, 0:1], None, ALU.mult).then_inc(s_b0p, 1)
            pool.tensor_scalar(b0_t[:, 1, :], b0_r[:, 0, :].bitcast(F32), row_id[:, 1:2], None,
                               ALU.mult).then_inc(s_b0p, 1)
            pool.wait_ge(s_b0p, 5)
            pool.tensor_tensor(b0_r[:, 1, :], b0_t[:, 0, :], b0_t[:, 1, :], ALU.add).then_inc(s_b0r, 1)
            iota(iota_key[:, :], [[1, 512]], 0, s_b0p)

        @block.vector
        def _(dve):
            v = nc.vector
            chain = [0]

            def mark(ins):
                chain[0] += 1
                ins.then_inc(s_v, 1)

            def link(ins):
                mark(ins)
                dve.wait_ge(s_v, chain[0])

            def in_pairs(ap):
                return ap.rearrange("p (k two) -> p k two", two=2).unsqueeze(1)

            dve.wait_ge(s_dst, 16)
            blocks = dst_flat[:, :].rearrange("p (b e) -> p b e", e=BLK)
            mark(v.tensor_reduce(blk[:, 0, 0, :], blocks, AX_X, ALU.max))
            link(v.tensor_reduce(blk[:, 0, 1, :], blocks, AX_X, ALU.min))
            link(v.tensor_scalar(blk[:, 1], blk[:, 0], 3, None, ALU.logical_shift_right))
            link(v.tensor_copy(blk2[:, :, :, :], blk[:, 1].unsqueeze(3).broadcast_to([P, 2, NB, 2])))
            dve.wait_ge(s_const, NCONST)
            for a, op in ((0, ALU.is_gt), (1, ALU.is_ge)):
                v.tensor_tensor(below[:, a].rearrange("p b (k two) -> p b k two", two=2),
                                in_pairs(iota_16[:, :]).broadcast_to([P, NB, P // 2, 2]),
                                blk2[:, a].unsqueeze(2).broadcast_to([P, NB, P // 2, 2]), op).then_inc(s_below, 1)

            dve.wait_ge(s_wf, 16)
            link(v.tensor_reduce(w_top[:, 0:1], w_flat[:, :], AX_X, ALU.max, apply_absolute_value=True))
            dve.wait_ge(s_ident, 5)
            v.tensor_scalar(w_diag[:, :], ident[:, :], w_top[:, 0:1], None, ALU.mult).then_inc(s_diag, 1)

            dve.wait_ge(s_cnt, 1)
            link(v.tensor_copy(cnt[:, :, :], ps_m[:, 0, 0:6].rearrange("p (a b) -> p a b", a=2)))
            n_blk = cnt[:, :, 0]
            idx_sum, twice, good = chk[:, 0:2], chk[:, 2:4], chk[:, 4:6]
            mark(v.scalar_tensor_tensor(idx_sum, cnt[:, :, 1], float(NB), cnt[:, :, 2], ALU.mult, ALU.add))
            mark(v.tensor_tensor(chk[:, 6:7], cnt[:, 1, 0:1], cnt[:, 0, 0:1], ALU.subtract))
            link(v.scalar_tensor_tensor(twice, n_blk, 1.0, n_blk, ALU.subtract, ALU.mult))
            link(v.scalar_tensor_tensor(good, idx_sum, 2.0, twice, ALU.mult, ALU.is_equal))
            link(v.scalar_tensor_tensor(chk[:, 7:8], chk[:, 6:7], float(CAP // BLK), chk[:, 4:5], ALU.is_le, ALU.mult))
            v.tensor_tensor(in_order[:, :], chk[:, 7:8], chk[:, 5:6], ALU.mult).then_inc(s_ok, 1)
            link(v.tensor_scalar(chk[:, 8:9], cnt[:, 0, 0:1], float(BLK), float(E - CAP), ALU.mult, ALU.min))
            dve.wait_ge(s_okcnt, 1)
            link(v.tensor_scalar(chk[:, 9:10], ps_m[:, 1, 0:1], float(NW), None, ALU.is_ge))
            v.tensor_tensor(start[:, :], chk[:, 8:9], chk[:, 9:10], ALU.mult).then_inc(s_start, 1)
            v.tensor_copy(flag[:, :], chk[:, 9:10]).then_inc(s_start, 1)

            def statistics(k):
                t = slice(k * MT // 2, (k + 1) * MT // 2)
                for m in range(k * MT // 2, (k + 1) * MT // 2):
                    if m % 2 == 0:
                        dve.wait_ge(s_x[m // 2], 16)
                    mark(v.bn_stats(stats[:, m, :], xn[:, m, :]))
                dve.wait_ge(s_v, chain[0])
                for m in range(k * MT // 2, (k + 1) * MT // 2):
                    mark(v.bn_aggr(mv[:, m, :], stats[:, m, :]))
                dve.wait_ge(s_v, chain[0])
                v.tensor_scalar(ntn[:, 0, t], mv[:, t, 1], EPS, None, ALU.add).then_inc(s_var, 1)

            def inverse_root(k):
                t = slice(k * MT // 2, (k + 1) * MT // 2)
                dve.wait_ge(s_std, k + 1)
                link(v.reciprocal(rstd[:, t], std[:, t]))
                link(v.tensor_tensor(ntn[:, 1, t], rstd[:, t], rstd[:, t], ALU.mult))
                link(v.tensor_tensor(ntn[:, 1, t], ntn[:, 1, t], ntn[:, 0, t], ALU.mult))
                link(v.tensor_scalar(ntn[:, 1, t], ntn[:, 1, t], -0.5, 1.5, ALU.mult, ALU.add))
                link(v.tensor_tensor(rstd[:, t], rstd[:, t], ntn[:, 1, t], ALU.mult))
                v.scalar_tensor_tensor(negm[:, t], mv[:, t, 0], -1.0, rstd[:, t], ALU.mult, ALU.mult).then_inc(s_rstd, 1)

            statistics(0)
            dve.wait_ge(s_wrep, 1)
            link(v.tensor_reduce(w_top[:, 1:2], ps_g[:, 0, 0:P], AX_X, ALU.max))
            link(v.tensor_scalar(w_top[:, 2:3], w_top[:, 1:2], TINY, None, ALU.max))
            link(v.tensor_scalar(w_top[:, 3:4].bitcast(I32), w_top[:, 2:3].bitcast(I32), 0x7F800000, None,
                                 ALU.bitwise_and))
            link(v.tensor_scalar(w_unscale[:, :], w_top[:, 3:4], 1.0 / TOP, None, ALU.mult))
            v.reciprocal(w_scale[:, :], w_unscale[:, :]).then_inc(s_wrep, 1)
            inverse_root(0)

            dve.wait_ge(s_gsd, 32)
            mark(v.tensor_scalar(s_int[:, 0, :], g_src, P - 1, None, ALU.bitwise_and))
            mark(v.tensor_scalar(s_int[:, 1, :], g_src, 7, None, ALU.logical_shift_right))
            link(v.tensor_scalar(d8, g_dst, win_base[:, :], float(MT), ALU.subtract, ALU.mult))
            v.tensor_copy(edge4[:, S_LO, :], s_int[:, 0, :]).then_inc(s_edge, 1)
            v.tensor_tensor(edge4[:, KEY, :], d8, s_int[:, 1, :], ALU.add).then_inc(s_edge, 1)
            dve.wait_ge(s_gw, 16)
            dve.wait_ge(s_wrep, 2)
            v.tensor_scalar(edge4[:, W_HI, :], g_w, w_scale[:, :], None, ALU.mult).then_inc(s_edge, 1)
            dve.wait_ge(s_edge, 3)
            v.scalar_tensor_tensor(edge4[:, W_LO, :], g_w, w_scale[:, :], edge4[:, W_HI, :], ALU.mult,
                                   ALU.subtract).then_inc(s_edge, 1)

            statistics(1)

            def onehots(h, b, reused):
                cols = pairs[:, :, bass.ds(h * HC, HC), :]
                if reused:
                    dve.wait_ge(s_built, h - 1)
                v.tensor_tensor(oh_lo[:, b].rearrange("p c (k two) -> p c k two", two=2),
                                in_pairs(iota_16[:, :]).broadcast_to([P, HC, P // 2, 2]),
                                cols[:, S_LO].unsqueeze(2).broadcast_to([P, HC, P // 2, 2]),
                                ALU.is_equal).then_inc(s_onehot, 1)
                v.tensor_tensor(oh_key[:, b].rearrange("p c (k two) -> p c k two", two=2),
                                in_pairs(iota_16[:, 0:KEYS]).broadcast_to([P, HC, KEYS // 2, 2]),
                                cols[:, KEY].unsqueeze(2).broadcast_to([P, HC, KEYS // 2, 2]),
                                ALU.is_equal).then_inc(s_onehot, 1)

            def weighted(h, b):
                cols = pairs[:, :, bass.ds(h * HC, HC), :]
                dve.wait_ge(s_onehot, 2 * h + 2)
                for part in range(2):
                    v.tensor_tensor(wkey[:, b, part].rearrange("p c (k two) -> p c k two", two=2),
                                    oh_key[:, b].rearrange("p c (k two) -> p c k two", two=2),
                                    cols[:, W_HI + part].unsqueeze(2).broadcast_to([P, HC, KEYS // 2, 2]),
                                    ALU.mult).then_inc(s_wk, 1)

            def factors(h, b, reused=True):
                onehots(h, b, reused)
                weighted(h, b)

            def sup_low(m):
                dve.wait_ge(s_suphi, m + 1)
                v.tensor_tensor(sup_lo[:, m, :], ps_g[:, m % 2, :], sup_hi[:, m, :].bitcast(F32),
                                ALU.subtract).then_inc(s_suplo, 1)

            def at_low(h, par, b):
                dve.wait_ge(s_athi, h + 1)
                d = slice(b * HD, (b + 1) * HD)
                v.scalar_tensor_tensor(at_lo[:, par, :, d].rearrange("p s d -> p d s"),
                                       ps_a[:, par, b, :].rearrange("p (d s) -> p d s", s=MT), w_unscale[:, :],
                                       at_hi[:, par, :, d].bitcast(F32).rearrange("p s d -> p d s"),
                                       ALU.mult, ALU.subtract).then_inc(s_atlo, 1)

            def general_factors(h):
                with dve.Fori(0, EP) as e:
                    step = h * EP + e
                    dve.wait_ge(s_gen_mm, step + 1)
                    v.tensor_scalar(gen_oh, iota_16[:, :], gen_lo[:, bass.ds(e, 1)], None,
                                    ALU.is_equal).then_inc(s_gen_f, 1)
                    dve.wait_ge(s_gen_key, h + 1)
                    v.tensor_scalar(gen_rhs, iota_key[:, :], gen_key[:, bass.ds(e, 1)], w_flat[:, bass.ds(e, 1)],
                                    ALU.is_equal, ALU.mult).then_inc(s_gen_f, 1)
                dve.wait_ge(s_gen_f, 2 * (h + 1) * EP)
                v.tensor_scalar(gen_key, gen_key, -512.0, None, ALU.add).then_inc(s_gen_key, 1)

            dve.wait_ge(s_start, 2)
            order_reg = dve.value_load(flag[0:1, 0:1], min_val=0, max_val=1)
            before_branch = chain[0]
            with dve.If(order_reg == 1):
                sup_low(0)
                dve.wait_ge(s_pairs, 2)
                onehots(0, 0, False)
                inverse_root(1)
                sup_low(1)
                dve.wait_ge(s_pairs, 4)
                weighted(0, 0)
                for h in range(1, NH):
                    onehots(h, h % 2, h >= 2)
                    if h + 1 < MT:
                        sup_low(h + 1)
                    weighted(h, h % 2)
                    for done in LOW_AFTER[h]:
                        at_low(done, done // 2 % 2, done % 2)
                for done in LOW_AFTER[NH]:
                    at_low(done, done // 2 % 2, done % 2)
            with dve.Else():
                chain[0] = before_branch
                inverse_root(1)
                dve.wait_ge(s_sf, 16)
                dve.wait_ge(s_b0p, 6)
                v.tensor_scalar(gen_int[:, 0, :], src_flat[:, :], P - 1, None, ALU.bitwise_and).then_inc(s_gen_v, 1)
                v.tensor_scalar(gen_int[:, 1, :], src_flat[:, :], 7, None,
                                ALU.logical_shift_right).then_inc(s_gen_v, 1)
                dve.wait_ge(s_gen_v, 2)
                v.tensor_copy(gen_lo, gen_int[:, 0, :]).then_inc(s_gen_v, 1)
                v.scalar_tensor_tensor(gen_key, dst_flat[:, :], float(MT), gen_int[:, 1, :],
                                       ALU.mult, ALU.add).then_inc(s_gen_key, 1)
                v.tensor_scalar(w_flat[:, :], w_flat[:, :], w_scale[:, :], None, ALU.mult).then_inc(s_gen_v, 1)
                dve.wait_ge(s_gen_v, 4)
                for m in range(MT):
                    sup_low(m)
                with dve.Fori(0, NG // 2) as p:
                    for par in range(2):
                        for b in range(2):
                            general_factors(4 * p + 2 * par + b)
                        for b in range(2):
                            at_low(4 * p + 2 * par + b, par, b)

            dve.wait_ge(s_c, NG * MT)
            v.tensor_reduce(chk[:, 0:MT], c_part[:, :, :].rearrange("p g s -> p s g"), AX_X, ALU.add).then_inc(s_csum, 1)
            dve.wait_ge(s_csum, 1)
            v.tensor_scalar(c_sum[:, :], chk[:, 0:MT], w_unscale[:, :], None, ALU.mult).then_inc(s_csum, 1)
            dve.wait_ge(s_csum, 2)
            dve.wait_ge(s_built, NH)
            for i in range(MT):
                dve.wait_ge(s_h1, i + 1)
                if i == 0:
                    v.tensor_scalar(acc, h1[:, 0, :], c_sum[:, 0:1], None, ALU.mult).then_inc(s_acc, 1)
                else:
                    dve.wait_ge(s_acc, i)
                    v.scalar_tensor_tensor(acc, h1[:, i, :], c_sum[:, i:i + 1], acc, ALU.mult,
                                           ALU.add).then_inc(s_acc, 1)

            def repeat(k):
                v.tensor_copy(rep[:, k], col[:, k, :].unsqueeze(2).broadcast_to([P, FT, Q])).then_inc(s_rep, 1)

            dve.wait_ge(s_colp, 1)
            v.tensor_copy(rep[:, 0], ps_m[:, 0, 0:FT].unsqueeze(2).broadcast_to([P, FT, Q])).then_inc(s_rep, 1)
            dve.wait_ge(s_col, 1)
            repeat(1)
            for k in (2, 3):
                dve.wait_ge(s_colp, k + 1)
                v.tensor_scalar(rep[:, k], ps_m[:, 1, (k - 1) * FT:k * FT].unsqueeze(2).broadcast_to([P, FT, Q]), 0.0, None,
                                ALU.max).then_inc(s_rep, 1)
            dve.wait_ge(s_finp, 2)
            dve.wait_ge(s_rowsum, 1)
            v.scalar_tensor_tensor(row, ps_a[:, 1, 0, :], 0.0, row_s, ALU.max, ALU.add).then_inc(s_row, 1)
            dve.wait_ge(s_row, 1)
            for m in range(MT):
                v.tensor_tensor(xn[:, m, :], xn[:, m, :], row, ALU.add).then_inc(s_y, 1)

        @block.scalar
        def _(act):
            a = nc.scalar
            def root(k):
                t = slice(k * MT // 2, (k + 1) * MT // 2)
                act.wait_ge(s_var, k + 1)
                a.activation(std[:, t], ntn[:, 0, t], ACT.Sqrt).then_inc(s_std, 1)

            def normalise(m):
                act.wait_ge(s_rstd, m // (MT // 2) + 1)
                if m >= 2:
                    act.wait_ge(s_h0tp, m - 1)
                a.activation(h0[:, m % 2, :], xn[:, m, :], ACT.Relu, bias=negm[:, m:m + 1],
                             scale=rstd[:, m:m + 1]).then_inc(s_h0, 1)

            def h0t_out(m):
                act.wait_ge(s_h0tp, m + 1)
                if m >= 2:
                    act.wait_ge(s_supp, m - 1)
                a.activation(h0t[:, m % 2, :], ps_m[:, m % 2, :], ACT.Copy).then_inc(s_h0t, 1)

            def sup_high(m):
                act.wait_ge(s_supp, m + 1)
                a.activation(sup_hi[:, m, :], ps_g[:, m % 2, :], ACT.Copy).then_inc(s_suphi, 1)

            def edge_values(r):
                act.wait_ge(s_etr, r + 2 - r % 2)
                half = ps_a[:, 0, r // 2, :].bitcast(F16)[:, r % 2 * CAP:r % 2 * CAP + CAP]
                a.activation(pairs[:, r].rearrange("p (w c) two -> p w c two", c=CH),
                             half.rearrange("p (c w) -> p w c", c=CH).unsqueeze(3).broadcast_to([P, NW, CH, 2]),
                             ACT.Copy).then_inc(s_pairs, 1)

            def at_high(h, par, b, i, reused=True):
                act.wait_ge(s_built, h + 1)
                if reused and b == 0:
                    act.wait_ge(s_agg, i - 1)
                a.activation(at_hi[:, par, :, b * HD:(b + 1) * HD].rearrange("p s d -> p d s"),
                             ps_a[:, par, b, :].rearrange("p (d s) -> p d s", s=MT), ACT.Copy,
                             scale=w_unscale[:, :]).then_inc(s_athi, 1)

            def column_sums(i, par, first=False):
                act.wait_ge(s_atlo, 2 * i + 2)
                if not first:
                    act.wait_ge(s_c, MT * i)
                for s in range(MT):
                    a.activation(c_junk[:, s, :], ps_a[:, par].rearrange("p b (d s) -> p (b d) s", s=MT)[:, :, s],
                                 ACT.Copy, accum_out=c_part[:, bass.ds(i, 1), s]).then_inc(s_c, 1)

            def h1_out(i, par):
                act.wait_ge(s_agg, i + 1)
                a.activation(h1[:, bass.ds(i, 1), :], ps_g[:, par:par + 1, :], ACT.Relu).then_inc(s_h1, 1)

            root(0)
            act.wait_ge(s_start, 2)
            order_reg = act.value_load(flag[0:1, 0:1], min_val=0, max_val=1)
            act.wait_ge(s_wrep, 2)
            normalise(0)
            normalise(1)
            h0t_out(0)
            normalise(2)
            h0t_out(1)
            normalise(3)
            act.wait_ge(s_b0, 32)
            a.activation(b0_r[:, 0, :], b0_sb[:, :], ACT.Copy).then_inc(s_b0r, 1)
            sup_high(0)
            h0t_out(2)
            with act.If(order_reg == 1):
                for r in range(4):
                    edge_values(r)
                root(1)
                for m in range(2, MT + 1):
                    if m + 2 < MT:
                        normalise(m + 2)
                    sup_high(m - 1)
                    if m + 1 < MT:
                        h0t_out(m + 1)
                    if 3 <= m < 7:
                        at_high(m - 3, (m - 3) // 2, (m - 3) % 2, 0, False)
                    if m == 5:
                        column_sums(0, 0, True)
                    if m == 7:
                        column_sums(1, 1)
                with act.Fori(1, NG // 2) as p:
                    for par in range(2):
                        i = 2 * p + par
                        for b in range(2):
                            at_high(2 * i + b, par, b, i)
                        h1_out(i - 2, par)
                        column_sums(i, par)
            with act.Else():
                root(1)
                for m in range(2, MT + 1):
                    if m + 2 < MT:
                        normalise(m + 2)
                    sup_high(m - 1)
                    if m + 1 < MT:
                        h0t_out(m + 1)
                for i in range(2):
                    for b in range(2):
                        at_high(2 * i + b, i, b, i, False)
                    column_sums(i, i, i == 0)
                with act.Fori(1, NG // 2) as p:
                    for par in range(2):
                        i = 2 * p + par
                        h1_out(i - 2, par)
                        for b in range(2):
                            at_high(2 * i + b, par, b, i)
                        column_sums(i, par)
            h1_out(NG - 2, 0)
            h1_out(NG - 1, 1)

            act.wait_ge(s_rowp, 1)
            a.activation(rows, ps_g[:, 1, :], ACT.Copy).then_inc(s_rows, 1)
            act.wait_ge(s_colp, 2)
            a.activation(col[:, 1, :], ps_m[:, 1, 0:FT], ACT.Sigmoid, scale=1.0 / N).then_inc(s_col, 1)
            act.wait_ge(s_rowp, 2)
            a.activation(rows, ps_g[:, 0, :], ACT.Copy).then_inc(s_rows, 1)
            act.wait_ge(s_rowp, 3)
            a.activation(rows_g, ps_a[:, 0, 1, :], ACT.Copy).then_inc(s_rowsg, 1)
            act.wait_ge(s_rowp, 4)
            a.activation(rows, ps_g[:, 1, :], ACT.Copy).then_inc(s_rows, 1)
            act.wait_ge(s_finp, 1)
            a.activation(row_s, ps_a[:, 0, 0, :], ACT.Copy).then_inc(s_rowsum, 1)
            act.wait_ge(s_rowp, 5)
            a.activation(rows, ps_g[:, 0, :], ACT.Copy).then_inc(s_rows, 1)

        @block.tensor
        def _(pe):
            mm = nc.tensor.matmul
            pe.wait_ge(s_const, NCONST)
            for a in range(2):
                pe.wait_ge(s_below, a + 1)
                for b in range(NB):
                    last = mm(ps_m[:, 0, 3 * a:3 * a + 3], below[:, a, b, :], blk_cols[:, b, :], start=b == 0,
                              stop=b == NB - 1)
            last.then_inc(s_cnt, 1)
            pe.wait_ge(s_diag, 1)
            mm(ps_g[:, 0, 0:P], ones_32[:, :], w_diag[:, :], start=True, stop=True).then_inc(s_wrep, 1)
            pe.wait_ge(s_ok, 1)
            mm(ps_m[:, 1, 0:1], ones_16[:, :], in_order[:, :], start=True, stop=True).then_inc(s_okcnt, 1)

            def transpose_h0(m):
                pe.wait_ge(s_h0, m + 1)
                if m >= 2:
                    pe.wait_ge(s_h0t, m - 1)
                for f in range(FT):
                    last = nc.tensor.transpose(ps_m[:, m % 2, f * P:(f + 1) * P], h0[:, m % 2, f * P:(f + 1) * P],
                                               ident[:, :])
                last.then_inc(s_h0tp, 1)

            def support(m):
                if m == 0:
                    pe.wait_ge(s_w0, 16)
                pe.wait_ge(s_h0t, m + 1)
                if m >= 2:
                    pe.wait_ge(s_suplo, m - 1)
                for f in range(FT):
                    last = mm(ps_g[:, m % 2, :], h0t[:, m % 2, f * P:(f + 1) * P], w_sb["W0"][:, f, :],
                              start=f == 0, stop=f == FT - 1)
                last.then_inc(s_supp, 1)

            def transpose_edges(r):
                pe.wait_ge(s_edge, r + 1)
                half = ps_a[:, 0, r // 2, :].bitcast(F16)
                for c in range(CH):
                    o = r % 2 * CAP + c * P
                    last = nc.tensor.transpose(half[:, o:o + P], edge4[:, r, c * P:(c + 1) * P], ident_16[:, :])
                last.then_inc(s_etr, 1)

            def build(h):
                b, par = h % 2, h // 2 % 2
                pe.wait_ge(s_onehot, 2 * h + 2)
                pe.wait_ge(s_wk, 2 * h + 2)
                if h >= 4:
                    pe.wait_ge(s_c, MT * (h // 2 - 1))
                for wdw in range(HC // CH):
                    for c in range(CH):
                        for part in range(2):
                            last = mm(ps_a[:, par, b, wdw * KEYS:(wdw + 1) * KEYS], oh_lo[:, b, wdw * CH + c, :],
                                      wkey[:, b, part, wdw * CH + c, :], start=c == 0 and part == 0,
                                      stop=c == CH - 1 and part == 1)
                last.then_inc(s_built, 1)

            def aggregate(i, par, reused=True):
                pe.wait_ge(s_atlo, 2 * i + 2)
                if reused:
                    pe.wait_ge(s_h1, i - 1)
                o = ps_g[:, par, :]
                mm(o, ones_r[:, :], b0_r[:, 1, :], start=True, stop=False)
                for s in range(MT):
                    mm(o, at_hi[:, par, s, :], sup_hi[:, s, :], start=False, stop=False)
                    mm(o, at_hi[:, par, s, :], sup_lo[:, s, :], start=False, stop=False)
                    last = mm(o, at_lo[:, par, s, :], sup_hi[:, s, :], start=False, stop=s == MT - 1)
                last.then_inc(s_agg, 1)

            def general_build(h, par, b, i, reused):
                if reused:
                    pe.wait_ge(s_c, MT * (i - 1))
                pe.wait_ge(s_gen_f, 2 * h * EP + 2)
                mm(ps_a[:, par, b, :], gen_oh, gen_rhs, start=True, stop=False,
                   skip_group_check=True).then_inc(s_gen_mm, 1)
                with pe.Fori(1, EP) as e:
                    pe.wait_ge(s_gen_f, 2 * h * EP + 2 * e + 2)
                    mm(ps_a[:, par, b, :], gen_oh, gen_rhs, start=False, stop=True,
                       skip_group_check=True).then_inc(s_gen_mm, 1)
                pe.wait_ge(s_gen_mm, (h + 1) * EP + 1)
                pe.sem_inc(s_built, 1)

            pe.wait_ge(s_ident, 5)
            pe.wait_ge(s_start, 2)
            order_reg = pe.value_load(flag[0:1, 0:1], min_val=0, max_val=1)
            pe.wait_ge(s_wrep, 2)
            transpose_h0(0)
            transpose_h0(1)
            support(0)
            transpose_h0(2)
            with pe.If(order_reg == 1):
                for r in range(4):
                    transpose_edges(r)
                support(1)
                for m in range(2, MT):
                    if m + 1 < MT:
                        transpose_h0(m + 1)
                    support(m)
                    if m == 2:
                        pe.wait_ge(s_pairs, 4)
                    build(m - 2)
                pe.wait_ge(s_ones, 3 + FT)
                pe.wait_ge(s_b0r, 2)
                pe.wait_ge(s_suplo, MT)
                for step, i in PE_ORDER:
                    if step == "build":
                        build(i)
                    else:
                        aggregate(i, i % 2, i >= 2)
            with pe.Else():
                support(1)
                for m in range(2, MT):
                    if m + 1 < MT:
                        transpose_h0(m + 1)
                    support(m)
                pe.wait_ge(s_ones, 3 + FT)
                pe.wait_ge(s_b0r, 2)
                pe.wait_ge(s_suplo, MT)
                pe.sem_inc(s_gen_mm, 1)
                for i in range(2):
                    for b in range(2):
                        general_build(2 * i + b, i, b, i, False)
                    aggregate(i, i, False)
                with pe.Fori(1, NG // 2) as p:
                    for par in range(2):
                        i = 2 * p + par
                        for b in range(2):
                            general_build(2 * i + b, par, b, i, True)
                        aggregate(i, par)

            one = ones_32[0:1, 0:1]
            cols_p = ps_m[:, 1, :]

            def row_layer(o, k, wt):
                pe.wait_ge(s_rep, k + 1)
                for f in range(FT):
                    last = mm(o[f * Q:(f + 1) * Q, :], rep[:, k, f, :], wt[:, f, :], start=True, stop=True)
                last.then_inc(s_rowp, 1)

            def to_column(o, n):
                pe.wait_ge(s_rows, n)
                for q in range(FT):
                    last = mm(o[:, q:q + 1], rows[:, q * P:(q + 1) * P], sel[:, 0:1], start=False, stop=True,
                              skip_group_check=True)
                last.then_inc(s_colp, 1)

            def to_row(o, ready, n, sums, part):
                pe.wait_ge(ready, n)
                mm(o, sums[:, :], part, start=False, stop=True).then_inc(s_finp, 1)

            pe.wait_ge(s_wts, 16 * 9)
            pe.wait_ge(s_c, MT * NG)
            mm(ps_a[:, 0, 0, :], ones_32[0:1, :], b_sb["gbs"][:, :], start=True, stop=False)
            mm(ps_a[:, 1, 0, :], ones_32[0:1, :], b_sb["gb3"][:, :], start=True, stop=False)
            for k, (bias, unit) in enumerate(((b_sb["b1"], node_count[:, :]), (b_sb["gb1"], one), (b_sb["gb2"], one))):
                for q in range(FT):
                    mm(cols_p[:, k * FT + q:k * FT + q + 1], bias[:, q * P:(q + 1) * P], unit,
                       start=k == 0 and q == 0, stop=False, skip_group_check=True)
            pe.wait_ge(s_h1, NG)
            pe.wait_ge(s_acc, MT)
            for q in range(FT):
                last = mm(ps_m[:, 0, q:q + 1], acc[:, q * P:(q + 1) * P], ones_32[:, 0:1], start=True, stop=True)
            last.then_inc(s_colp, 1)
            row_layer(ps_g[:, 1, :], 0, w_sb["W1"])
            to_column(cols_p[:, 0:FT], 1)
            row_layer(ps_g[:, 0, :], 1, w_sb["gW1"])
            pe.wait_ge(s_gws, 16)
            row_layer(ps_a[:, 0, 1, :], 1, w_gWs)
            to_column(cols_p[:, FT:2 * FT], 2)
            row_layer(ps_g[:, 1, :], 2, w_sb["gW2"])
            to_row(ps_a[:, 0, 0, :], s_rowsg, 1, sel, rows_g)
            to_column(cols_p[:, 2 * FT:3 * FT], 3)
            row_layer(ps_g[:, 0, :], 3, w_sb["gW3"])
            to_row(ps_a[:, 1, 0, :], s_rows, 4, sel, rows)


_INS = ['x', 'src', 'dst', 'edge_weight', 'L0_gnn_W0', 'L0_gnn_b0', 'L0_gnn_W1', 'L0_gnn_b1', 'L0_gnn_gW1',
        'L0_gnn_gb1', 'L0_gnn_gW2', 'L0_gnn_gb2', 'L0_gnn_gW3', 'L0_gnn_gb3', 'L0_gnn_gWs', 'L0_gnn_gbs']
_OUTS = [((1024, 512), 'float32')]


def kernel(**inputs):
    import numpy as _np
    import concourse.bacc as _bacc
    from concourse import mybir as _mybir
    from concourse.bass_utils import run_bass_kernel_spmd as _run

    nc = _bacc.Bacc("TRN2", target_bir_lowering=False, num_devices=1)
    arrays, args = {}, []
    for name in _INS:
        a = _np.ascontiguousarray(inputs[name])
        arrays[f"in_{name}_dram"] = a
        args.append(nc.dram_tensor(f"in_{name}_dram", a.shape, _mybir.dt.from_np(a.dtype), kind="ExternalInput").ap())
    for i, (shape, dtype) in enumerate(_OUTS):
        dt = _mybir.dt.from_np(_np.dtype(dtype))
        args.append(nc.dram_tensor(f"out_{i}_dram", shape, dt, kind="ExternalOutput").ap())
    gnn_block(nc, *args)
    r = _run(nc, [arrays], core_ids=[0])
    return r.results[0]["out_0_dram"]
```

```python
import concourse.bass as bass
from concourse import mybir
from contextlib import ExitStack

F32 = mybir.dt.float32
I32 = mybir.dt.int32
U32 = mybir.dt.uint32
ALU = mybir.AluOpType
ACT = mybir.ActivationFunctionType
AX_X = mybir.AxisListType.X

F16 = mybir.dt.float16
F32R = mybir.dt.float32r
P = 128


def gnn_block(nc, x, src, dst, edge_weight, W0, b0, W1, b1, gW1, gb1, gW2, gb2, gW3, gb3, gWs, gbs, out):
    N, D = x.shape
    E = src.shape[0]
    MT = N // P
    FT = D // P
    WIN = 8
    NW = N // WIN
    CH = 3
    CAP = CH * P
    KEYS = WIN * MT
    NG = N // P
    NH = 2 * NG
    HD = P // 2
    HC = HD // WIN * CH
    EP = E // P
    BLK = 24
    NB = EP // BLK
    Q = P // FT
    EPS = 1e-5
    TOP = 2.0 ** 14
    TINY = 2.0 ** -100
    NORM = (slice(0, 2), slice(2, MT))
    LOW_POOL = 4
    PE_ORDER = [("product", 0), ("build", 6), ("build", 7), ("product", 1), ("build", 8), ("product", 2),
                ("build", 9), ("build", 10), ("product", 3), ("build", 11), ("product", 4), ("build", 12),
                ("build", 13), ("product", 5), ("build", 14), ("build", 15), ("product", 6), ("product", 7)]
    assert NW == P and KEYS * (HD // WIN) == 512 and EP % BLK == 0 and CAP % BLK == 0 and NG == MT == 8

    ctx = ExitStack()
    with ctx:
        def sb(name, shape, dt=F32):
            return ctx.enter_context(nc.sbuf_tensor(name, shape, dt))

        def ps(name, shape, dt=F32):
            return ctx.enter_context(nc.psum_tensor(name, shape, dt))

        def sem(name):
            return ctx.enter_context(nc.semaphore(name))

        iota_16 = sb("iota_16", [P, P], F16)
        win_base = sb("win_base", [P, 1])
        ident_16 = sb("ident_16", [P, P], F16)
        ident = sb("ident", [P, P])
        ones_16 = sb("ones_16", [P, P], F16)
        ones_32 = sb("ones_32", [P, P])
        ones_r = sb("ones_r", [2, P], F32R)
        sel = sb("sel", [P, P])
        node_count = sb("node_count", [1, P // FT])
        blk_cols = sb("blk_cols", [P, NB, 3], F16)
        row_id = sb("row_id", [2, 2])
        dst_flat = sb("dst_flat", [P, EP], I32)
        src_flat = sb("src_flat", [P, EP], I32)
        w_flat = sb("w_flat", [P, EP])
        blk = sb("blk", [P, 2, 2, NB], I32)
        blk2 = sb("blk2", [P, 2, NB, 2], F16)
        below = sb("below", [P, 2, NB, P], F16)
        cnt = sb("cnt", [P, 2, 3])
        chk = sb("chk", [P, 16])
        in_order = sb("in_order", [P, 1], F16)
        start = sb("start", [P, 1], U32)
        flag = sb("flag", [P, 1], I32)
        w_top = sb("w_top", [P, 4])
        w_diag = sb("w_diag", [P, P])
        w_scale = sb("w_scale", [P, 1])
        w_unscale = sb("w_unscale", [P, 1])
        S_LO, KEY, W_HI, W_LO = range(4)
        pairs = sb("pairs", [P, 4, NW * CH, 2], F16)
        oh_lo = sb("oh_lo", [P, 2, HC, P], F16)
        oh_key = sb("oh_key", [P, 2, HC, KEYS], F16)
        wkey = sb("wkey", [P, 2, 2, HC, KEYS], F16)
        at_hi = sb("at_hi", [P, 2, MT, P], F32R)
        at_all = sb("at_all", [P, 2, MT, HD])
        at_lo = sb("at_lo", [P, 2, MT, P], F32R)
        c_part = sb("c_part", [P, NG, MT])
        c_sum = sb("c_sum", [P, MT])
        c_junk = sb("c_junk", [P, MT, P], F16)
        xn = sb("xn", [P, MT, D])
        x_sums = sb("x_sums", [P, 2, 4])
        stats = sb("stats", [P, MT, 6])
        mv = sb("mv", [P, MT, 2])
        std = sb("std", [P, MT])
        rstd = sb("rstd", [P, MT])
        ntn = sb("ntn", [P, 2, MT])
        negm = sb("negm", [P, MT])
        h0 = sb("h0", [P, 2, D])
        h0t_hi = sb("h0t_hi", [P, 2, D], F32R)
        sup_hi = sb("sup_hi", [P, MT, D], F32R)
        sup_lo = sb("sup_lo", [P, MT, D], F32R)
        w_sb = {k: sb(f"w_{k}", [P, FT, D]) for k in ("W0", "W1", "gW1", "gW2")}
        b_sb = {k: sb(f"b_{k}", [1, D]) for k in ("b1", "gb1", "gb2", "gb3", "gbs")}
        b0_sb = sb("b0_sb", [2, D])
        b0_r = sb("b0_r", [2, 2, D], F32R)
        b0_t = sb("b0_t", [2, 2, D])
        with ExitStack() as early:
            w0_hi = early.enter_context(nc.sbuf_tensor("w0_hi", [P, FT, D], F32R))
            w0_lo = early.enter_context(nc.sbuf_tensor("w0_lo", [P, FT, D], F32R))
            h0t_lo = early.enter_context(nc.sbuf_tensor("h0t_lo", [P, 2, D], F32R))
            h0t_all = early.enter_context(nc.sbuf_tensor("h0t_all", [P, 2, D], F32))
            sup_all = early.enter_context(nc.sbuf_tensor("sup_all", [P, 2, D], F32))
        h1 = sb("h1", [P, MT, D])
        w_sb["gW3"] = sb("w_gW3", [P, FT, D])
        rep = sb("rep", [P, 4, FT, Q])

        words = wkey[:, :, :, :, :].rearrange("p a b c k -> p (a b c k)")
        g_src = words[:, 0:2 * CAP].bitcast(I32)
        g_dst = words[:, 2 * CAP:4 * CAP].bitcast(I32)
        g_w = words[:, 4 * CAP:6 * CAP].bitcast(F32)
        s_int = words[:, 6 * CAP:10 * CAP].bitcast(I32).rearrange("p (a e) -> p a e", a=2)
        d8 = words[:, 10 * CAP:12 * CAP].bitcast(F32)
        edge4 = words[:, 12 * CAP:16 * CAP].rearrange("p (a e) -> p a e", a=4)
        gen_words = below[:, :, :, :].rearrange("p a b t -> p (a b t)")
        gen_int = gen_words[:, 0:4 * EP].bitcast(I32).rearrange("p (a e) -> p a e", a=2)
        gen_lo = gen_words[:, 4 * EP:6 * EP].bitcast(F32)
        gen_key = gen_words[:, 6 * EP:8 * EP].bitcast(F32)
        iota_key = pairs[:, :, :, :].rearrange("p a c two -> p (a c two)")[:, 0:2 * 512].bitcast(F32)
        gen_oh = oh_lo[:, 0, 0:2, :].rearrange("p c k -> p (c k)").bitcast(F32)
        gen_rhs = oh_lo[:, 1, 0:8, :].rearrange("p c k -> p (c k)").bitcast(F32)
        late = oh_lo[:, :, :, :].rearrange("p a c k -> p (a c k)").bitcast(F32)
        acc = late[:, 0:D]
        row = late[:, 2 * D:3 * D]
        row_s = late[:, D:2 * D]
        rows, rows_g = h0[:, 0, :], h0[:, 1, :]
        w_gWs = w_sb["W0"]

        ps_a = ps("ps_a", [P, 2, 2, 512])
        ps_g = ps("ps_g", [P, 2, 512])
        ps_m = ps("ps_m", [P, 2, 512])

        s_dst, s_wf, s_sf, s_w0, s_b0, s_wts, s_gws, s_gw3 = (sem(k) for k in (
            "s_dst", "s_wf", "s_sf", "s_w0", "s_b0", "s_wts", "s_gws", "s_gw3"))
        s_x = [sem(f"s_x{k}") for k in range(MT // 2)]
        s_const, s_ident, s_ones, s_b0p, s_b0r = (sem(k) for k in ("s_const", "s_ident", "s_ones", "s_b0p", "s_b0r"))
        s_below, s_diag, s_wrep, s_cnt, s_ok, s_okcnt, s_start = (sem(k) for k in (
            "s_below", "s_diag", "s_wrep", "s_cnt", "s_ok", "s_okcnt", "s_start"))
        s_gsd, s_gw, s_edge, s_etr, s_pairs = (sem(k) for k in ("s_gsd", "s_gw", "s_edge", "s_etr", "s_pairs"))
        s_onehot, s_wk, s_built, s_athi, s_atlo, s_c = (sem(k) for k in (
            "s_onehot", "s_wk", "s_built", "s_athi", "s_atlo", "s_c"))
        s_sums, s_var, s_std, s_rstd, s_h0, s_h0tp, s_h0thi, s_h0tlo, s_h0tall = (sem(k) for k in (
            "s_sums", "s_var", "s_std", "s_rstd", "s_h0", "s_h0tp", "s_h0thi", "s_h0tlo", "s_h0tall"))
        s_w0hi, s_w0lo, s_supp, s_suphi, s_suplo = (sem(k) for k in (
            "s_w0hi", "s_w0lo", "s_supp", "s_suphi", "s_suplo"))
        s_agg, s_h1, s_csum, s_acc = (sem(k) for k in ("s_agg", "s_h1", "s_csum", "s_acc"))
        s_table, s_colp, s_rep, s_rowp, s_rows_a, s_rows_b, s_rowsg, s_finp, s_rowsum, s_row, s_y, s_out = (
            sem(k) for k in ("s_table", "s_colp", "s_rep", "s_rowp", "s_rows_a", "s_rows_b", "s_rowsg",
                             "s_finp", "s_rowsum", "s_row", "s_y", "s_out"))
        s_gen_f, s_gen_mm, s_gen_key, s_gen_v = (sem(k) for k in ("s_gen_f", "s_gen_mm", "s_gen_key", "s_gen_v"))
        s_v = sem("s_v")

        block = ctx.enter_context(nc.Block())
        NCONST = 6

        @block.sync
        def _(sp):
            sp.dma_start(dst_flat[:, :], dst.rearrange("(p e) -> p e", p=P)).then_inc(s_dst, 16)
            sp.dma_start(w_flat[:, :], edge_weight.rearrange("(p e) -> p e", p=P)).then_inc(s_wf, 16)
            xv = x.rearrange("(m p) d -> p m d", p=P)
            for m in range(0, MT, 2):
                if m == MT // 2:
                    sp.dma_start(w_sb["W0"][:, :, :], W0.rearrange("(f p) d -> p f d", p=P)).then_inc(s_w0, 16)
                if m == MT - 2:
                    sp.wait_ge(s_std, 1)
                sp.dma_start(xn[:, m:m + 2, :], xv[:, m:m + 2, :]).then_inc(s_x[m // 2], 16)
            for r in range(2):
                sp.dma_start(b0_sb[r:r + 1, :], b0.rearrange("(a d) -> a d", a=1)).then_inc(s_b0, 16)
            sp.wait_ge(s_gsd, 32)
            sp.wait_ge(s_gw, 16)
            sp.dma_start(src_flat[:, :], src.rearrange("(p e) -> p e", p=P)).then_inc(s_sf, 16)
            for k, v in (("b1", b1), ("gb1", gb1), ("gb2", gb2), ("gb3", gb3), ("gbs", gbs)):
                sp.dma_start(b_sb[k][:, :], v.rearrange("(a d) -> a d", a=1)).then_inc(s_wts, 16)
            for k, v in (("W1", W1), ("gW1", gW1), ("gW2", gW2)):
                sp.dma_start(w_sb[k][:, :, :], v.rearrange("(f p) d -> p f d", p=P)).then_inc(s_wts, 16)
            sp.wait_ge(s_w0lo, FT)
            sp.dma_start(w_gWs[:, :, :], gWs.rearrange("(f p) d -> p f d", p=P)).then_inc(s_gws, 16)
            sp.wait_ge(s_supp, MT)
            sp.wait_ge(s_suplo, MT)
            sp.dma_start(w_sb["gW3"][:, :, :], gW3.rearrange("(f p) d -> p f d", p=P)).then_inc(s_gw3, 16)
            ov = out.rearrange("(m p) d -> p m d", p=P)
            for m in range(MT):
                sp.wait_ge(s_y, m + 1)
                sp.dma_start(ov[:, m, :], xn[:, m, :]).then_inc(s_out, 16)
            sp.wait_ge(s_out, 16 * MT)

        @block.gpsimd
        def _(pool):
            def iota(o, pattern, mult, s):
                pool.iota(o, pattern, base=0, channel_multiplier=mult,
                          allow_small_or_imprecise_dtypes=True).then_inc(s, 1)

            iota(iota_16[:, :], [[1, P]], 0, s_const)
            pool.memset(blk_cols[:, :, 0], 1.0).then_inc(s_const, 1)
            iota(blk_cols[:, :, 1], [[0, NB]], 1, s_const)
            iota(blk_cols[:, :, 2], [[1, NB]], 0, s_const)
            pool.memset(ones_16[:, :], 1.0).then_inc(s_const, 1)
            iota(win_base[:, :], [[0, 1]], WIN, s_const)
            pool.memset(ident[:, :], 0.0).then_inc(s_ident, 1)
            pool.memset(ones_32[:, :], 1.0).then_inc(s_ident, 1)
            pool.memset(ident_16[:, :], 0.0).then_inc(s_ident, 1)
            pool.wait_ge(s_ident, 3)
            for m in (ident, ident_16):
                pool.affine_select(out=m[:, :], in_=m[:, :], compare_op=ALU.not_equal, fill=1.0, base=0,
                                   pattern=[[-1, P]], channel_multiplier=1).then_inc(s_ident, 1)
            pool.memset(node_count[:, :], float(N)).then_inc(s_ones, 1)
            pool.memset(ones_r[:, :].bitcast(F32), 1.0).then_inc(s_ones, 1)
            pool.memset(sel[:, :], 0.0).then_inc(s_ones, 1)
            pool.wait_ge(s_ones, 3)
            for f in range(FT):
                pool.memset(sel[f * Q:f * Q + 1, :], 1.0).then_inc(s_ones, 1)
            iota(row_id[:, 0:1], [[0, 1]], 1, s_b0p)
            pool.wait_ge(s_b0p, 1)
            pool.tensor_scalar(row_id[:, 1:2], row_id[:, 0:1], -1.0, 1.0, ALU.mult, ALU.add).then_inc(s_b0p, 1)
            pool.wait_ge(s_start, 2)
            for g, v, s in ((g_src, src, s_gsd), (g_dst, dst, s_gsd), (g_w, edge_weight, s_gw)):
                pool.indirect_dma_start(g, None, v.rearrange("(e one) -> e one", one=1),
                                        bass.IndirectOffsetOnAxis(ap=start[:, :], axis=0)).then_inc(s, 16)
            for f in range(FT // 2):
                pool.wait_ge(s_w0hi, f + 1)
                pool.tensor_tensor(w0_lo[:, f, :], w_sb["W0"][:, f, :], w0_hi[:, f, :].bitcast(F32),
                                   ALU.subtract).then_inc(s_w0lo, 1)
            pool.wait_ge(s_b0, 32)
            pool.wait_ge(s_b0r, 1)
            pool.tensor_tensor(b0_t[:, 0, :], b0_sb[:, :], b0_r[:, 0, :].bitcast(F32), ALU.subtract).then_inc(s_b0p, 1)
            pool.wait_ge(s_b0p, 3)
            pool.tensor_scalar(b0_t[:, 0, :], b0_t[:, 0, :], row_id[:, 0:1], None, ALU.mult).then_inc(s_b0p, 1)
            pool.tensor_scalar(b0_t[:, 1, :], b0_r[:, 0, :].bitcast(F32), row_id[:, 1:2], None,
                               ALU.mult).then_inc(s_b0p, 1)
            pool.wait_ge(s_b0p, 5)
            pool.tensor_tensor(b0_r[:, 1, :], b0_t[:, 0, :], b0_t[:, 1, :], ALU.add).then_inc(s_b0r, 1)

            def sup_low(m):
                pool.wait_ge(s_suphi, 2 * m + 2)
                pool.tensor_tensor(sup_lo[:, m, :], sup_all[:, m % 2, :], sup_hi[:, m, :].bitcast(F32),
                                   ALU.subtract).then_inc(s_suplo, 1)

            def h0t_low(m):
                pool.wait_ge(s_h0tlo, m)
                pool.wait_ge(s_h0tall, m + 1 - LOW_POOL)
                pool.wait_ge(s_supp, m - 1)
                pool.tensor_tensor(h0t_lo[:, m % 2, :], h0t_all[:, m % 2, :], h0t_hi[:, m % 2, :].bitcast(F32),
                                   ALU.subtract).then_inc(s_h0tlo, 1)

            def at_low(h, par, b):
                pool.wait_ge(s_athi, 2 * h + 2)
                d = slice(b * HD, (b + 1) * HD)
                pool.tensor_tensor(at_lo[:, par, :, d], at_all[:, b, :, :], at_hi[:, par, :, d].bitcast(F32),
                                   ALU.subtract).then_inc(s_atlo, 1)

            order_reg = pool.value_load(flag[0:1, 0:1], min_val=0, max_val=1)
            with pool.If(order_reg == 1):
                for m in range(MT):
                    if LOW_POOL <= m + 2 < MT:
                        h0t_low(m + 2)
                    sup_low(m)
                    if 3 <= m < 7:
                        at_low(m - 3, (m - 3) // 2 % 2, (m - 3) % 2)
                for h in range(4, NH):
                    at_low(h, h // 2 % 2, h % 2)
            with pool.Else():
                iota(iota_key, [[1, 512]], 0, s_b0p)
                for m in range(MT):
                    if LOW_POOL <= m + 2 < MT:
                        h0t_low(m + 2)
                    sup_low(m)
                with pool.Fori(0, NG // 2) as p:
                    for par in range(2):
                        for b in range(2):
                            at_low(4 * p + 2 * par + b, par, b)

        @block.vector
        def _(dve):
            v = nc.vector
            chain = [0]

            def mark(ins):
                chain[0] += 1
                ins.then_inc(s_v, 1)

            def link(ins):
                mark(ins)
                dve.wait_ge(s_v, chain[0])

            def in_pairs(ap):
                return ap.rearrange("p (k two) -> p k two", two=2).unsqueeze(1)

            dve.wait_ge(s_dst, 16)
            blocks = dst_flat[:, :].rearrange("p (b e) -> p b e", e=BLK)
            mark(v.tensor_reduce(blk[:, 0, 0, :], blocks, AX_X, ALU.max))
            link(v.tensor_reduce(blk[:, 0, 1, :], blocks, AX_X, ALU.min))
            link(v.tensor_scalar(blk[:, 1], blk[:, 0], 3, None, ALU.logical_shift_right))
            link(v.tensor_copy(blk2[:, :, :, :], blk[:, 1].unsqueeze(3).broadcast_to([P, 2, NB, 2])))
            dve.wait_ge(s_const, NCONST)
            for a, op in ((0, ALU.is_gt), (1, ALU.is_ge)):
                v.tensor_tensor(below[:, a].rearrange("p b (k two) -> p b k two", two=2),
                                in_pairs(iota_16[:, :]).broadcast_to([P, NB, P // 2, 2]),
                                blk2[:, a].unsqueeze(2).broadcast_to([P, NB, P // 2, 2]), op).then_inc(s_below, 1)

            dve.wait_ge(s_wf, 16)
            link(v.tensor_reduce(w_top[:, 0:1], w_flat[:, :], AX_X, ALU.max, apply_absolute_value=True))
            dve.wait_ge(s_ident, 5)
            v.tensor_scalar(w_diag[:, :], ident[:, :], w_top[:, 0:1], None, ALU.mult).then_inc(s_diag, 1)

            dve.wait_ge(s_cnt, 1)
            link(v.tensor_copy(cnt[:, :, :], ps_m[:, 0, 0:6].rearrange("p (a b) -> p a b", a=2)))
            n_blk = cnt[:, :, 0]
            idx_sum, twice, good = chk[:, 0:2], chk[:, 2:4], chk[:, 4:6]
            mark(v.scalar_tensor_tensor(idx_sum, cnt[:, :, 1], float(NB), cnt[:, :, 2], ALU.mult, ALU.add))
            mark(v.tensor_tensor(chk[:, 6:7], cnt[:, 1, 0:1], cnt[:, 0, 0:1], ALU.subtract))
            link(v.scalar_tensor_tensor(twice, n_blk, 1.0, n_blk, ALU.subtract, ALU.mult))
            link(v.scalar_tensor_tensor(good, idx_sum, 2.0, twice, ALU.mult, ALU.is_equal))
            link(v.scalar_tensor_tensor(chk[:, 7:8], chk[:, 6:7], float(CAP // BLK), chk[:, 4:5], ALU.is_le, ALU.mult))
            v.tensor_tensor(in_order[:, :], chk[:, 7:8], chk[:, 5:6], ALU.mult).then_inc(s_ok, 1)
            link(v.tensor_scalar(chk[:, 8:9], cnt[:, 0, 0:1], float(BLK), float(E - CAP), ALU.mult, ALU.min))
            dve.wait_ge(s_okcnt, 1)
            link(v.tensor_scalar(chk[:, 9:10], ps_m[:, 1, 0:1], float(NW), None, ALU.is_ge))
            v.tensor_tensor(start[:, :], chk[:, 8:9], chk[:, 9:10], ALU.mult).then_inc(s_start, 1)
            v.tensor_copy(flag[:, :], chk[:, 9:10]).then_inc(s_start, 1)

            def statistics(m):
                for t in (m, m + 1):
                    dve.wait_ge(s_x[m // 2], 16)
                    mark(v.bn_stats(stats[:, t, :], xn[:, t, :]))
                dve.wait_ge(s_v, chain[0])
                for t in (m, m + 1):
                    mark(v.bn_aggr(mv[:, t, :], stats[:, t, :]))

            def w0_low(f):
                dve.wait_ge(s_w0hi, f + 1)
                v.tensor_tensor(w0_lo[:, f, :], w_sb["W0"][:, f, :], w0_hi[:, f, :].bitcast(F32),
                                ALU.subtract).then_inc(s_w0lo, 1)

            def h0t_low(m):
                dve.wait_ge(s_h0thi, m + 1)
                if m >= 2:
                    dve.wait_ge(s_supp, m - 1)
                v.tensor_tensor(h0t_lo[:, m % 2, :], ps_m[:, m % 2, :], h0t_hi[:, m % 2, :].bitcast(F32),
                                ALU.subtract).then_inc(s_h0tlo, 1)

            def inverse_root(k):
                t = NORM[k]
                dve.wait_ge(s_std, k + 1)
                link(v.reciprocal(rstd[:, t], std[:, t]))
                link(v.tensor_tensor(ntn[:, 1, t], rstd[:, t], rstd[:, t], ALU.mult))
                link(v.tensor_tensor(ntn[:, 1, t], ntn[:, 1, t], ntn[:, 0, t], ALU.mult))
                link(v.tensor_scalar(ntn[:, 1, t], ntn[:, 1, t], -0.5, 1.5, ALU.mult, ALU.add))
                link(v.tensor_tensor(rstd[:, t], rstd[:, t], ntn[:, 1, t], ALU.mult))
                v.scalar_tensor_tensor(negm[:, t], mv[:, t, 0], -1.0, rstd[:, t], ALU.mult,
                                       ALU.mult).then_inc(s_rstd, 1)

            dve.wait_ge(s_wrep, 1)
            dve.wait_ge(s_sums, 6)
            v.tensor_scalar(ntn[:, 0, NORM[0]], x_sums[:, 1, 0:2], 1.0 / D, EPS, ALU.mult,
                            ALU.add).then_inc(s_var, 1)
            link(v.tensor_reduce(w_top[:, 1:2], ps_g[:, 0, 0:P], AX_X, ALU.max))
            link(v.tensor_scalar(w_top[:, 2:3], w_top[:, 1:2], TINY, None, ALU.max))
            link(v.tensor_scalar(w_top[:, 3:4].bitcast(I32), w_top[:, 2:3].bitcast(I32), 0x7F800000, None,
                                 ALU.bitwise_and))
            link(v.tensor_scalar(w_unscale[:, :], w_top[:, 3:4], 1.0 / TOP, None, ALU.mult))
            v.reciprocal(w_scale[:, :], w_unscale[:, :]).then_inc(s_wrep, 1)
            inverse_root(0)
            statistics(2)
            statistics(4)
            w0_low(2)
            w0_low(3)
            h0t_low(0)
            h0t_low(1)

            dve.wait_ge(s_gsd, 32)
            mark(v.tensor_scalar(s_int[:, 0, :], g_src, P - 1, None, ALU.bitwise_and))
            mark(v.tensor_scalar(s_int[:, 1, :], g_src, 7, None, ALU.logical_shift_right))
            link(v.tensor_scalar(d8, g_dst, win_base[:, :], float(MT), ALU.subtract, ALU.mult))
            v.tensor_copy(edge4[:, S_LO, :], s_int[:, 0, :]).then_inc(s_edge, 1)
            v.tensor_tensor(edge4[:, KEY, :], d8, s_int[:, 1, :], ALU.add).then_inc(s_edge, 1)
            dve.wait_ge(s_gw, 16)
            dve.wait_ge(s_wrep, 2)
            v.tensor_scalar(edge4[:, W_HI, :], g_w, w_scale[:, :], None, ALU.mult).then_inc(s_edge, 1)
            dve.wait_ge(s_edge, 3)
            v.scalar_tensor_tensor(edge4[:, W_LO, :], g_w, w_scale[:, :], edge4[:, W_HI, :], ALU.mult,
                                   ALU.subtract).then_inc(s_edge, 1)

            dve.wait_ge(s_v, chain[0])
            v.tensor_scalar(ntn[:, 0, 2:6], mv[:, 2:6, 1], EPS, None, ALU.add).then_inc(s_var, 1)
            dve.wait_ge(s_sums, 11)
            v.tensor_scalar(ntn[:, 0, 6:8], x_sums[:, 1, 2:4], 1.0 / D, EPS, ALU.mult, ALU.add).then_inc(s_var, 1)
            inverse_root(1)

            def onehot_lo(h, b, reused):
                cols = pairs[:, :, bass.ds(h * HC, HC), :]
                if reused:
                    dve.wait_ge(s_built, h - 1)
                v.tensor_tensor(oh_lo[:, b].rearrange("p c (k two) -> p c k two", two=2),
                                in_pairs(iota_16[:, :]).broadcast_to([P, HC, P // 2, 2]),
                                cols[:, S_LO].unsqueeze(2).broadcast_to([P, HC, P // 2, 2]),
                                ALU.is_equal).then_inc(s_onehot, 1)

            def onehot_key(h, b):
                cols = pairs[:, :, bass.ds(h * HC, HC), :]
                v.tensor_tensor(oh_key[:, b].rearrange("p c (k two) -> p c k two", two=2),
                                in_pairs(iota_16[:, 0:KEYS]).broadcast_to([P, HC, KEYS // 2, 2]),
                                cols[:, KEY].unsqueeze(2).broadcast_to([P, HC, KEYS // 2, 2]),
                                ALU.is_equal).then_inc(s_onehot, 1)

            def weighted(h, b):
                cols = pairs[:, :, bass.ds(h * HC, HC), :]
                dve.wait_ge(s_onehot, 2 * h + 2)
                for part in range(2):
                    v.tensor_tensor(wkey[:, b, part].rearrange("p c (k two) -> p c k two", two=2),
                                    oh_key[:, b].rearrange("p c (k two) -> p c k two", two=2),
                                    cols[:, W_HI + part].unsqueeze(2).broadcast_to([P, HC, KEYS // 2, 2]),
                                    ALU.mult).then_inc(s_wk, 1)

            def general_factors(h):
                with dve.Fori(0, EP) as e:
                    step = h * EP + e
                    dve.wait_ge(s_gen_mm, step + 1)
                    v.tensor_scalar(gen_oh, iota_16[:, :], gen_lo[:, bass.ds(e, 1)], None,
                                    ALU.is_equal).then_inc(s_gen_f, 1)
                    dve.wait_ge(s_gen_key, h + 1)
                    v.tensor_scalar(gen_rhs, iota_key, gen_key[:, bass.ds(e, 1)], w_flat[:, bass.ds(e, 1)],
                                    ALU.is_equal, ALU.mult).then_inc(s_gen_f, 1)
                dve.wait_ge(s_gen_f, 2 * (h + 1) * EP)
                v.tensor_scalar(gen_key, gen_key, -512.0, None, ALU.add).then_inc(s_gen_key, 1)

            dve.wait_ge(s_start, 2)
            order_reg = dve.value_load(flag[0:1, 0:1], min_val=0, max_val=1)
            before_branch = chain[0]
            with dve.If(order_reg == 1):
                dve.wait_ge(s_pairs, 2)
                onehot_lo(0, 0, False)
                h0t_low(2)
                onehot_key(0, 0)
                dve.wait_ge(s_pairs, 4)
                weighted(0, 0)
                h0t_low(3)
                for h in range(1, NH):
                    onehot_lo(h, h % 2, h >= 2)
                    onehot_key(h, h % 2)
                    if h + 3 < min(LOW_POOL, MT):
                        h0t_low(h + 3)
                    weighted(h, h % 2)
            with dve.Else():
                chain[0] = before_branch
                dve.wait_ge(s_sf, 16)
                dve.wait_ge(s_b0p, 6)
                v.tensor_scalar(gen_int[:, 0, :], src_flat[:, :], P - 1, None, ALU.bitwise_and).then_inc(s_gen_v, 1)
                v.tensor_scalar(gen_int[:, 1, :], src_flat[:, :], 7, None,
                                ALU.logical_shift_right).then_inc(s_gen_v, 1)
                dve.wait_ge(s_gen_v, 2)
                v.tensor_copy(gen_lo, gen_int[:, 0, :]).then_inc(s_gen_v, 1)
                v.scalar_tensor_tensor(gen_key, dst_flat[:, :], float(MT), gen_int[:, 1, :],
                                       ALU.mult, ALU.add).then_inc(s_gen_key, 1)
                v.tensor_scalar(w_flat[:, :], w_flat[:, :], w_scale[:, :], None, ALU.mult).then_inc(s_gen_v, 1)
                dve.wait_ge(s_gen_v, 4)
                for m in range(2, LOW_POOL):
                    h0t_low(m)
                with dve.Fori(0, NG // 2) as p:
                    for par in range(2):
                        for b in range(2):
                            general_factors(4 * p + 2 * par + b)

            dve.wait_ge(s_c, NG * MT)
            v.tensor_reduce(chk[:, 0:MT], c_part[:, :, :].rearrange("p g s -> p s g"), AX_X,
                            ALU.add).then_inc(s_csum, 1)
            dve.wait_ge(s_csum, 1)
            v.tensor_scalar(c_sum[:, :], chk[:, 0:MT], w_unscale[:, :], None, ALU.mult).then_inc(s_csum, 1)
            dve.wait_ge(s_csum, 2)
            dve.wait_ge(s_built, NH)
            for i in range(NG - 1):
                dve.wait_ge(s_h1, i + 1)
                if i == 0:
                    v.tensor_scalar(acc, h1[:, 0, :], c_sum[:, 0:1], None, ALU.mult).then_inc(s_acc, 1)
                else:
                    dve.wait_ge(s_acc, i)
                    v.scalar_tensor_tensor(acc, h1[:, i, :], c_sum[:, i:i + 1], acc, ALU.mult,
                                           ALU.add).then_inc(s_acc, 1)

            def rows_out(o, n):
                dve.wait_ge(s_rowp, n)
                v.tensor_copy(rows[:, D // 2:D], o).then_inc(s_rows_b, 1)

            dve.wait_ge(s_table, 1)
            dve.wait_ge(s_colp, 1)
            v.tensor_copy(rep[:, 0], ps_a[:, 0, 0, 0:FT].unsqueeze(2).broadcast_to([P, FT, Q])).then_inc(s_rep, 1)
            rows_out(ps_m[:, 1, 0:D // 2], 2)
            rows_out(ps_g[:, 1, 0:D // 2], 4)
            for k, o in ((2, ps_m[:, 1, 0:D // 2]), (3, ps_g[:, 1, 0:D // 2])):
                dve.wait_ge(s_colp, k + 1)
                v.tensor_scalar(rep[:, k], ps_a[:, 0, 1, (k - 1) * FT:k * FT].unsqueeze(2).broadcast_to([P, FT, Q]),
                                0.0, None, ALU.max).then_inc(s_rep, 1)
                rows_out(o, 2 * k + 4)
            dve.wait_ge(s_rowsum, 1)
            for half in range(2):
                cols = slice(half * D // 2, (half + 1) * D // 2)
                dve.wait_ge(s_finp, 2 + half)
                v.scalar_tensor_tensor(row[:, cols], ps_a[:, 1, half, cols], 0.0, row_s[:, cols], ALU.max,
                                       ALU.add).then_inc(s_row, 1)
            dve.wait_ge(s_row, 2)
            for m in range(MT):
                v.tensor_tensor(xn[:, m, :], xn[:, m, :], row, ALU.add).then_inc(s_y, 1)

        @block.scalar
        def _(act):
            a = nc.scalar
            def root(k):
                t = NORM[k]
                act.wait_ge(s_var, 1 + 2 * k)
                a.activation(std[:, t], ntn[:, 0, t], ACT.Sqrt).then_inc(s_std, 1)

            def normalise(m):
                act.wait_ge(s_rstd, 1 if m < NORM[1].start else 2)
                if m >= 2:
                    act.wait_ge(s_h0tp, m - 1)
                a.activation(h0[:, m % 2, :], xn[:, m, :], ACT.Relu, bias=negm[:, m:m + 1],
                             scale=rstd[:, m:m + 1]).then_inc(s_h0, 1)

            def h0t_out(m):
                act.wait_ge(s_h0tp, m + 1)
                if m >= 2:
                    act.wait_ge(s_supp, m - 1)
                a.activation(h0t_hi[:, m % 2, :], ps_m[:, m % 2, :], ACT.Copy).then_inc(s_h0thi, 1)
                if m >= LOW_POOL:
                    if m >= LOW_POOL + 2:
                        act.wait_ge(s_h0tlo, m - 1)
                    a.activation(h0t_all[:, m % 2, :], ps_m[:, m % 2, :], ACT.Copy).then_inc(s_h0tall, 1)

            def sup_high(m):
                act.wait_ge(s_supp, m + 1)
                a.activation(sup_hi[:, m, :], ps_g[:, m % 2, :], ACT.Copy).then_inc(s_suphi, 1)
                if m >= 2:
                    act.wait_ge(s_suplo, m - 1)
                a.activation(sup_all[:, m % 2, :], ps_g[:, m % 2, :], ACT.Copy).then_inc(s_suphi, 1)

            def edge_values(r):
                act.wait_ge(s_etr, r + 2 - r % 2)
                half = ps_a[:, 0, r // 2, :].bitcast(F16)[:, r % 2 * CAP:r % 2 * CAP + CAP]
                a.activation(pairs[:, r].rearrange("p (w c) two -> p w c two", c=CH),
                             half.rearrange("p (c w) -> p w c", c=CH).unsqueeze(3).broadcast_to([P, NW, CH, 2]),
                             ACT.Copy).then_inc(s_pairs, 1)

            def at_high(h, par, b, i, reused=True):
                act.wait_ge(s_built, h + 1)
                if reused and b == 0:
                    act.wait_ge(s_agg, i - 1)
                a.activation(at_hi[:, par, :, b * HD:(b + 1) * HD].rearrange("p s d -> p d s"),
                             ps_a[:, par, b, :].rearrange("p (d s) -> p d s", s=MT), ACT.Copy,
                             scale=w_unscale[:, :]).then_inc(s_athi, 1)
                if reused or h >= 2:
                    act.wait_ge(s_atlo, h - 1)
                a.activation(at_all[:, b, :, :].rearrange("p s d -> p d s"),
                             ps_a[:, par, b, :].rearrange("p (d s) -> p d s", s=MT), ACT.Copy,
                             scale=w_unscale[:, :]).then_inc(s_athi, 1)

            def column_sums(i, par, first=False):
                if not first:
                    act.wait_ge(s_c, MT * i)
                for s in range(MT):
                    a.activation(c_junk[:, s, :], ps_a[:, par].rearrange("p b (d s) -> p (b d) s", s=MT)[:, :, s],
                                 ACT.Copy, accum_out=c_part[:, bass.ds(i, 1), s]).then_inc(s_c, 1)

            def h1_out(i, par):
                act.wait_ge(s_agg, i + 1)
                a.activation(h1[:, bass.ds(i, 1), :], ps_g[:, par:par + 1, :], ACT.Relu).then_inc(s_h1, 1)

            def w0_high(f):
                a.activation(w0_hi[:, f, :], w_sb["W0"][:, f, :], ACT.Copy).then_inc(s_w0hi, 1)

            def sum_up(m, slot, before):
                t, o = slice(m, m + 2), slice(slot, slot + 2)
                act.wait_ge(s_x[m // 2], 16)
                for k in range(2):
                    a.activation(sup_hi[:, 2 * slot + k, :], xn[:, m + k, :], ACT.Copy,
                                 accum_out=x_sums[:, 0, slot + k:slot + k + 1]).then_inc(s_sums, 1)
                act.wait_ge(s_sums, before + 2)
                a.activation(mv[:, t, 0], x_sums[:, 0, o], ACT.Copy, scale=1.0 / D).then_inc(s_sums, 1)
                act.wait_ge(s_sums, before + 3)
                for k in range(2):
                    a.activation(sup_hi[:, 2 * slot + 2 + k, :], xn[:, m + k, :], ACT.Square, bias=mv[:, m + k, 0:1],
                                 scale=-1.0, accum_out=x_sums[:, 1, slot + k:slot + k + 1]).then_inc(s_sums, 1)

            act.wait_ge(s_const, NCONST)
            a.activation(std[0:1, 0:1], ones_16[0:1, 0:1], ACT.Sqrt).then_inc(s_sums, 1)
            sum_up(0, 0, 1)
            root(0)
            act.wait_ge(s_w0, 16)
            w0_high(0)
            w0_high(1)
            order_reg = act.value_load(flag[0:1, 0:1], min_val=0, max_val=1)
            act.wait_ge(s_wrep, 2)
            normalise(0)
            normalise(1)
            w0_high(2)
            w0_high(3)
            h0t_out(0)
            h0t_out(1)
            sum_up(6, 2, 6)
            act.wait_ge(s_b0, 32)
            a.activation(b0_r[:, 0, :], b0_sb[:, :], ACT.Copy).then_inc(s_b0r, 1)
            root(1)
            with act.If(order_reg == 1):
                edge_values(0)
                edge_values(1)
                normalise(2)
                normalise(3)
                edge_values(2)
                h0t_out(2)
                sup_high(0)
                edge_values(3)
                normalise(4)
                sup_high(1)
                h0t_out(3)
                normalise(5)
                for m in range(2, MT):
                    sup_high(m)
                    if m + 2 < MT:
                        h0t_out(m + 2)
                    if m + 4 < MT:
                        normalise(m + 4)
                    if m < 6:
                        at_high(m - 2, (m - 2) // 2, m % 2, 0, False)
                    if m == 4:
                        column_sums(0, 0, True)
                    if m == 6:
                        column_sums(1, 1)
                with act.Fori(1, NG // 2) as p:
                    for par in range(2):
                        i = 2 * p + par
                        for b in range(2):
                            at_high(2 * i + b, par, b, i)
                        h1_out(i - 2, par)
                        column_sums(i, par)
            with act.Else():
                normalise(2)
                normalise(3)
                sup_high(0)
                h0t_out(2)
                normalise(4)
                sup_high(1)
                h0t_out(3)
                normalise(5)
                for m in range(2, MT):
                    sup_high(m)
                    if m + 2 < MT:
                        h0t_out(m + 2)
                    if m + 4 < MT:
                        normalise(m + 4)
                for i in range(2):
                    for b in range(2):
                        at_high(2 * i + b, i, b, i, False)
                    column_sums(i, i, i == 0)
                with act.Fori(1, NG // 2) as p:
                    for par in range(2):
                        i = 2 * p + par
                        h1_out(i - 2, par)
                        for b in range(2):
                            at_high(2 * i + b, par, b, i)
                        column_sums(i, par)
            h1_out(NG - 2, 0)
            a.activation(rep[0:1, 0, 0, 0:1], w_unscale[0:1, :], ACT.Sigmoid).then_inc(s_table, 1)
            h1_out(NG - 1, 1)

            def rows_out(o, n):
                act.wait_ge(s_rowp, n)
                a.activation(rows[:, 0:D // 2], o, ACT.Copy).then_inc(s_rows_a, 1)

            rows_out(ps_m[:, 0, 0:D // 2], 1)
            act.wait_ge(s_colp, 2)
            a.activation(rep[:, 1], ps_a[:, 0, 1, 0:FT].unsqueeze(2).broadcast_to([P, FT, Q]), ACT.Sigmoid,
                         scale=1.0 / N).then_inc(s_rep, 1)
            rows_out(ps_g[:, 0, 0:D // 2], 3)
            for half in range(2):
                act.wait_ge(s_rowp, 5 + half)
                a.activation(rows_g[:, half * D // 2:(half + 1) * D // 2], ps_a[:, 1, half, 0:D // 2],
                             ACT.Copy).then_inc(s_rowsg, 1)
            rows_out(ps_m[:, 0, 0:D // 2], 7)
            rows_out(ps_g[:, 0, 0:D // 2], 9)
            act.wait_ge(s_finp, 1)
            a.activation(row_s, ps_a[:, 0, 0, :], ACT.Copy).then_inc(s_rowsum, 1)

        @block.tensor
        def _(pe):
            mm = nc.tensor.matmul
            pe.wait_ge(s_const, NCONST)
            for a in range(2):
                pe.wait_ge(s_below, a + 1)
                for b in range(NB):
                    last = mm(ps_m[:, 0, 3 * a:3 * a + 3], below[:, a, b, :], blk_cols[:, b, :], start=b == 0,
                              stop=b == NB - 1)
            last.then_inc(s_cnt, 1)
            pe.wait_ge(s_diag, 1)
            mm(ps_g[:, 0, 0:P], ones_32[:, :], w_diag[:, :], start=True, stop=True).then_inc(s_wrep, 1)
            pe.wait_ge(s_ok, 1)
            mm(ps_m[:, 1, 0:1], ones_16[:, :], in_order[:, :], start=True, stop=True).then_inc(s_okcnt, 1)

            def keep_warm(bank, n):
                for _ in range(n):
                    mm(bank[:, D // 2:D // 2 + P], ones_16[:, :], iota_16[:, :], start=True, stop=True)

            def transpose_h0(m):
                pe.wait_ge(s_h0, m + 1)
                if m >= 2:
                    pe.wait_ge(s_h0tlo, m - 1)
                for f in range(FT):
                    last = nc.tensor.transpose(ps_m[:, m % 2, f * P:(f + 1) * P], h0[:, m % 2, f * P:(f + 1) * P],
                                               ident[:, :])
                last.then_inc(s_h0tp, 1)

            def support(m):
                def products(h0t, w0, first=False, final=False):
                    for f in range(FT):
                        last = mm(ps_g[:, m % 2, :], h0t[:, m % 2, f * P:(f + 1) * P], w0[:, f, :],
                                  start=first and f == 0, stop=final and f == FT - 1)
                    return last

                pe.wait_ge(s_h0thi, m + 1)
                if m == 0:
                    pe.wait_ge(s_w0hi, FT)
                if m >= 2:
                    pe.wait_ge(s_suphi, 2 * m - 2)
                products(h0t_hi, w0_hi, first=True)
                pe.wait_ge(s_h0tlo, m + 1)
                products(h0t_lo, w0_hi)
                if m == 0:
                    pe.wait_ge(s_w0lo, FT)
                products(h0t_hi, w0_lo, final=True).then_inc(s_supp, 1)

            def transpose_edges(r):
                pe.wait_ge(s_edge, r + 1)
                half = ps_a[:, 0, r // 2, :].bitcast(F16)
                for c in range(CH):
                    o = r % 2 * CAP + c * P
                    last = nc.tensor.transpose(half[:, o:o + P], edge4[:, r, c * P:(c + 1) * P], ident_16[:, :])
                last.then_inc(s_etr, 1)

            def build(h):
                b, par = h % 2, h // 2 % 2
                pe.wait_ge(s_onehot, 2 * h + 2)
                pe.wait_ge(s_wk, 2 * h + 2)
                if h >= 4:
                    pe.wait_ge(s_c, MT * (h // 2 - 1))
                for wdw in range(HC // CH):
                    for c in range(CH):
                        for part in range(2):
                            last = mm(ps_a[:, par, b, wdw * KEYS:(wdw + 1) * KEYS], oh_lo[:, b, wdw * CH + c, :],
                                      wkey[:, b, part, wdw * CH + c, :], start=c == 0 and part == 0,
                                      stop=c == CH - 1 and part == 1)
                last.then_inc(s_built, 1)

            def aggregate(i, par, reused=True):
                pe.wait_ge(s_atlo, 2 * i + 2)
                if reused:
                    pe.wait_ge(s_h1, i - 1)
                o = ps_g[:, par, :]
                mm(o, ones_r[:, :], b0_r[:, 1, :], start=True, stop=False)
                for s in range(MT):
                    mm(o, at_hi[:, par, s, :], sup_hi[:, s, :], start=False, stop=False)
                    mm(o, at_hi[:, par, s, :], sup_lo[:, s, :], start=False, stop=False)
                    last = mm(o, at_lo[:, par, s, :], sup_hi[:, s, :], start=False, stop=s == MT - 1)
                last.then_inc(s_agg, 1)

            def general_build(h, par, b, i, reused):
                if reused:
                    pe.wait_ge(s_c, MT * (i - 1))
                pe.wait_ge(s_gen_f, 2 * h * EP + 2)
                mm(ps_a[:, par, b, :], gen_oh, gen_rhs, start=True, stop=False,
                   skip_group_check=True).then_inc(s_gen_mm, 1)
                with pe.Fori(1, EP) as e:
                    pe.wait_ge(s_gen_f, 2 * h * EP + 2 * e + 2)
                    mm(ps_a[:, par, b, :], gen_oh, gen_rhs, start=False, stop=True,
                       skip_group_check=True).then_inc(s_gen_mm, 1)
                pe.wait_ge(s_gen_mm, (h + 1) * EP + 1)
                pe.sem_inc(s_built, 1)

            def row_bias(o, bias, unit):
                for half in range(2):
                    mm(o[half * Q:(half + 1) * Q, half, 0:D // 2], unit, bias[:, half * D // 2:(half + 1) * D // 2],
                       start=True, stop=False, skip_group_check=True)

            def first_bias():
                pe.wait_ge(s_wts, 16 * 8)
                row_bias(ps_m, b_sb["b1"], node_count[:, :])

            pe.wait_ge(s_ident, 5)
            pe.wait_ge(s_start, 2)
            order_reg = pe.value_load(flag[0:1, 0:1], min_val=0, max_val=1)
            pe.wait_ge(s_wrep, 2)
            transpose_h0(0)
            transpose_h0(1)
            with pe.If(order_reg == 1):
                support(0)
                for r in range(4):
                    transpose_edges(r)
                support(1)
                transpose_h0(2)
                transpose_h0(3)
                for m in range(2, MT):
                    support(m)
                    if m + 2 < MT:
                        transpose_h0(m + 2)
                    if m == 2:
                        pe.wait_ge(s_pairs, 4)
                    build(m - 2)
                pe.wait_ge(s_ones, 3 + FT)
                pe.wait_ge(s_b0r, 2)
                first_bias()
                pe.wait_ge(s_suplo, MT)
                for step, i in PE_ORDER:
                    if step == "build":
                        build(i)
                    else:
                        aggregate(i, i % 2, i >= 2)
            with pe.Else():
                support(0)
                support(1)
                transpose_h0(2)
                transpose_h0(3)
                for m in range(2, MT):
                    support(m)
                    if m + 2 < MT:
                        transpose_h0(m + 2)
                pe.wait_ge(s_ones, 3 + FT)
                pe.wait_ge(s_b0r, 2)
                first_bias()
                pe.wait_ge(s_suplo, MT)
                pe.sem_inc(s_gen_mm, 1)
                for i in range(2):
                    for b in range(2):
                        general_build(2 * i + b, i, b, i, False)
                    aggregate(i, i, False)
                with pe.Fori(1, NG // 2) as p:
                    for par in range(2):
                        i = 2 * p + par
                        for b in range(2):
                            general_build(2 * i + b, par, b, i, True)
                        aggregate(i, par)

            def row_layer(o, k, wt):
                pe.wait_ge(s_rep, k + 1)
                for half in range(2):
                    for f in range(FT):
                        last = mm(o[f * Q:(f + 1) * Q, half, 0:D // 2], rep[:, k, f, :],
                                  wt[:, f, half * D // 2:(half + 1) * D // 2], start=f != half, stop=True,
                                  skip_group_check=True)
                    last.then_inc(s_rowp, 1)

            def to_column(o, n):
                for half, rows_ready in enumerate((s_rows_a, s_rows_b)):
                    pe.wait_ge(rows_ready, n)
                    for q in range(half * FT // 2, (half + 1) * FT // 2):
                        last = mm(o[:, q:q + 1], rows[:, q * P:(q + 1) * P], sel[:, 0:1], start=True, stop=True)
                last.then_inc(s_colp, 1)

            even, odd = ps_m, ps_g
            pe.wait_ge(s_c, MT * NG)
            pe.wait_ge(s_acc, NG - 1)
            for q in range(FT):
                mm(ps_a[:, 0, 0, q:q + 1], acc[:, q * P:(q + 1) * P], ones_32[:, 0:1], start=q == 0, stop=False,
                   skip_group_check=True)
            keep_warm(ps_a[:, 1, 0], 6)
            pe.wait_ge(s_h1, NG)
            for q in range(FT):
                last = mm(ps_a[:, 0, 0, q:q + 1], h1[:, NG - 1, q * P:(q + 1) * P], c_sum[:, NG - 1:NG], start=False,
                          stop=True, skip_group_check=True)
            last.then_inc(s_colp, 1)
            keep_warm(ps_a[:, 1, 0], 8)
            row_layer(even, 0, w_sb["W1"])
            row_bias(odd, b_sb["gb1"], ones_32[0:1, 0:Q])
            to_column(ps_a[:, 0, 1, 0:FT], 1)
            keep_warm(ps_a[:, 1, 0], 8)
            row_bias(ps_a[:, 1], b_sb["gbs"], ones_32[0:1, 0:Q])
            row_layer(odd, 1, w_sb["gW1"])
            pe.wait_ge(s_gws, 16)
            row_layer(ps_a[:, 1], 1, w_gWs)
            row_bias(even, b_sb["gb2"], ones_32[0:1, 0:Q])
            to_column(ps_a[:, 0, 1, FT:2 * FT], 2)
            keep_warm(odd[:, 0], 8)
            row_layer(even, 2, w_sb["gW2"])
            row_bias(odd, b_sb["gb3"], ones_32[0:1, 0:Q])
            to_column(ps_a[:, 0, 1, 2 * FT:3 * FT], 3)
            keep_warm(even[:, 0], 8)
            pe.wait_ge(s_gw3, 16)
            row_layer(odd, 3, w_sb["gW3"])
            pe.wait_ge(s_rowsg, 2)
            mm(ps_a[:, 0, 0, :], sel[:, :], rows_g, start=True, stop=True).then_inc(s_finp, 1)
            for half, rows_ready in enumerate((s_rows_a, s_rows_b)):
                pe.wait_ge(rows_ready, 4)
                o = slice(half * D // 2, (half + 1) * D // 2)
                mm(ps_a[:, 1, half, o], sel[:, :], rows[:, o], start=True, stop=True).then_inc(s_finp, 1)


_INS = ['x', 'src', 'dst', 'edge_weight', 'L0_gnn_W0', 'L0_gnn_b0', 'L0_gnn_W1', 'L0_gnn_b1', 'L0_gnn_gW1',
        'L0_gnn_gb1', 'L0_gnn_gW2', 'L0_gnn_gb2', 'L0_gnn_gW3', 'L0_gnn_gb3', 'L0_gnn_gWs', 'L0_gnn_gbs']
_OUTS = [((1024, 512), 'float32')]


def kernel(**inputs):
    import numpy as _np
    import concourse.bacc as _bacc
    from concourse import mybir as _mybir
    from concourse.bass_utils import run_bass_kernel_spmd as _run

    nc = _bacc.Bacc("TRN2", target_bir_lowering=False, num_devices=1)
    arrays, args = {}, []
    for name in _INS:
        a = _np.ascontiguousarray(inputs[name])
        arrays[f"in_{name}_dram"] = a
        args.append(nc.dram_tensor(f"in_{name}_dram", a.shape, _mybir.dt.from_np(a.dtype), kind="ExternalInput").ap())
    for i, (shape, dtype) in enumerate(_OUTS):
        dt = _mybir.dt.from_np(_np.dtype(dtype))
        args.append(nc.dram_tensor(f"out_{i}_dram", shape, dt, kind="ExternalOutput").ap())
    gnn_block(nc, *args)
    r = _run(nc, [arrays], core_ids=[0])
    return r.results[0]["out_0_dram"]
```
